# Optimizing a Trainium2 kernel written in Bass

```python
import numpy as np
import jax
import jax.numpy as jnp

def _softmax(x, axis=-1):
    return jax.nn.softmax(x, axis=axis)

def _gelu(x):
    return jax.nn.gelu(x, approximate=True)

def _silu(x):
    return jax.nn.silu(x)

def _sigmoid(x):
    return jax.nn.sigmoid(x)

def _layernorm(x, axis=-1, eps=1e-05):
    m = jnp.mean(x, axis=axis, keepdims=True)
    v = jnp.var(x, axis=axis, keepdims=True)
    return (x - m) / jnp.sqrt(v + eps)

def _scatter_add(tgt, idx, src, axis=0):
    return tgt.at[idx].add(src)

def _segment_sum(src, seg, n):
    return jax.ops.segment_sum(src, seg, n)
kernel_name = 'mk_lm_tower_d2_tok_ids1024_r4_96d724'

def setup_inputs(seed: int=0):
    np.random.seed(seed)
    _w = jnp.asarray

    def _rec_inputs():
        import jax
        import jax.numpy as jnp
        _rk = jax.random.key(seed)
        x = jax.random.randint(jax.random.fold_in(_rk, 1), (2, 1024), 0, 12564, jnp.int32)
        return x
    x = _rec_inputs()

    def _L0_tok_setup():
        import jax, jax.numpy as jnp
        import numpy as np
        VOCAB = 50257
        D_MODEL = 256
        BATCH = 4
        SEQ = 1024
        key = jax.random.key(seed)
        k_ids, k_w = jax.random.split(key)
        input = jax.random.randint(k_ids, (BATCH, SEQ), 0, VOCAB, dtype=jnp.int32)
        W = jax.random.normal(k_w, (D_MODEL, VOCAB), dtype=jnp.float32) * (1.0 / np.sqrt(VOCAB))
        return {'input': input, 'W': W}
    _L0_tok_all = _L0_tok_setup()
    _L0_tok_in = {k: v for k, v in _L0_tok_all.items() if k in ('W',)}
    del _L0_tok_all

    def _L0_attn_setup():
        import jax, jax.numpy as jnp
        import numpy as np
        THETA = 10000.0

        def _rope(x, pos):
            hd = x.shape[-1]
            inv_freq = 1.0 / THETA ** (jnp.arange(0, hd, 2, dtype=jnp.float32) / hd)
            ang = pos.astype(jnp.float32)[:, None] * inv_freq[None, :]
            cos, sin = (jnp.cos(ang), jnp.sin(ang))
            x1, x2 = (x[..., 0::2], x[..., 1::2])
            r1 = x1 * cos - x2 * sin
            r2 = x1 * sin + x2 * cos
            return jnp.stack([r1, r2], axis=-1).reshape(x.shape)
        key = jax.random.key(seed)
        ks = jax.random.split(key, 5)
        b, s, d = (2, 512, 256)
        scale = 0.02
        return {'x': jax.random.normal(ks[0], (b, s, d), dtype=jnp.float32), 'Wq': jax.random.normal(ks[1], (d, d), dtype=jnp.float32) * scale, 'Wk': jax.random.normal(ks[2], (d, d), dtype=jnp.float32) * scale, 'Wv': jax.random.normal(ks[3], (d, d), dtype=jnp.float32) * scale, 'Wo': jax.random.normal(ks[4], (d, d), dtype=jnp.float32) * scale}
    _L0_attn_all = _L0_attn_setup()
    _L0_attn_in = {k: v for k, v in _L0_attn_all.items() if k in ('Wq', 'Wk', 'Wv', 'Wo')}
    del _L0_attn_all

    def _L0_ffn_setup():
        import jax, jax.numpy as jnp
        import numpy as np
        D_MODEL = 256
        D1, D2 = (32, 32)
        F1, F2 = (64, 64)
        E = 64
        TOP_K = 2

        def kmoe(x_flat, W_router, A, B, scale, bias, d_in1, d_in2, d_out1, d_out2, top_k):
            logits = x_flat @ W_router.T
            vals, idx = jax.lax.top_k(logits, top_k)
            probs = jax.nn.softmax(vals, axis=-1)
            xs = x_flat.reshape(-1, d_in1, d_in2)
            Ag = A[idx]
            Bg = B[idx]
            Y = jnp.einsum('nkoi,nij,nkpj->nkop', Ag, xs, Bg)
            out = jnp.einsum('nkop,nk->nop', Y, probs).reshape(-1, d_out1 * d_out2)
            return out * scale + bias
        key = jax.random.key(seed)
        ks = jax.random.split(key, 12)
        s = 0.02
        return {'x': jax.random.normal(ks[0], (4, 512, D_MODEL), dtype=jnp.float32), 'W_up': jax.random.normal(ks[1], (E, D1 * D2), dtype=jnp.float32) * s, 'A_up': jax.random.normal(ks[2], (E, F1, D1), dtype=jnp.float32) * s, 'B_up': jax.random.normal(ks[3], (E, F2, D2), dtype=jnp.float32) * s, 'scale_up': jnp.ones((1,), dtype=jnp.float32), 'bias_up': jnp.zeros((F1 * F2,), dtype=jnp.float32), 'W_down': jax.random.normal(ks[4], (E, F1 * F2), dtype=jnp.float32) * s, 'A_down': jax.random.normal(ks[5], (E, D1, F1), dtype=jnp.float32) * s, 'B_down': jax.random.normal(ks[6], (E, D2, F2), dtype=jnp.float32) * s, 'scale_down': jnp.ones((1,), dtype=jnp.float32), 'bias_down': jnp.zeros((D1 * D2,), dtype=jnp.float32)}
    _L0_ffn_all = _L0_ffn_setup()
    _L0_ffn_in = {k: v for k, v in _L0_ffn_all.items() if k in ('W_up', 'A_up', 'B_up', 'scale_up', 'bias_up', 'W_down', 'A_down', 'B_down', 'scale_down', 'bias_down')}
    del _L0_ffn_all

    def _L1_attn_setup():
        import jax, jax.numpy as jnp
        import numpy as np
        D_MODEL = 256
        N_HEADS = 16
        HEAD_DIM = D_MODEL // N_HEADS
        ROPE_BASE = 10000.0

        def _rope_tables(T, dtype=jnp.float32):
            half = HEAD_DIM // 2
            inv_freq = 1.0 / ROPE_BASE ** (jnp.arange(0, HEAD_DIM, 2, dtype=jnp.float32) / HEAD_DIM)
            t = jnp.arange(T, dtype=jnp.float32)
            freqs = jnp.einsum('i,j->ij', t, inv_freq)
            return (jnp.cos(freqs).astype(dtype), jnp.sin(freqs).astype(dtype))

        def _apply_rotary(x, cos, sin):
            B, T, H, D = x.shape
            xr = x.reshape(B, T, H, D // 2, 2)
            x0, x1 = (xr[..., 0], xr[..., 1])
            c = cos[None, :, None, :]
            s = sin[None, :, None, :]
            out = jnp.stack([x0 * c - x1 * s, x0 * s + x1 * c], axis=-1)
            return out.reshape(B, T, H, D)
        key = jax.random.key(seed)
        ks = jax.random.split(key, 5)
        x = jax.random.normal(ks[0], (4, 256, D_MODEL), dtype=jnp.float32)
        init = 1.0 / np.sqrt(D_MODEL)
        Wq = jax.random.uniform(ks[1], (D_MODEL, D_MODEL), jnp.float32, -init, init)
        Wk = jax.random.uniform(ks[2], (D_MODEL, D_MODEL), jnp.float32, -init, init)
        Wv = jax.random.uniform(ks[3], (D_MODEL, D_MODEL), jnp.float32, -init, init)
        Wo = jax.random.uniform(ks[4], (D_MODEL, D_MODEL), jnp.float32, -init, init)
        return {'x': x, 'Wq': Wq, 'Wk': Wk, 'Wv': Wv, 'Wo': Wo}
    _L1_attn_all = _L1_attn_setup()
    _L1_attn_in = {k: v for k, v in _L1_attn_all.items() if k in ('Wq', 'Wk', 'Wv', 'Wo')}
    del _L1_attn_all

    def _L1_ffn_setup():
        import jax, jax.numpy as jnp
        import numpy as np
        B, N, C, H, REG = (1, 2309, 256, 16, 5)
        D = C // H
        key = jax.random.key(seed)
        k0, k1, k2, k3 = jax.random.split(key, 4)
        x = jax.random.normal(k0, (B, N, C), dtype=jnp.float32)
        g_info = jax.random.normal(k1, (12, 2, C), dtype=jnp.float32)
        W_qkv = jax.random.normal(k2, (C, 3 * C), dtype=jnp.float32) * 0.02
        W_proj = jax.random.normal(k3, (C, C), dtype=jnp.float32) * 0.02
        b_proj = jnp.zeros((C,), dtype=jnp.float32)
        return {'x': x, 'g_info': g_info, 'W_qkv': W_qkv, 'W_proj': W_proj, 'b_proj': b_proj}
    _L1_ffn_all = _L1_ffn_setup()
    _L1_ffn_in = {k: v for k, v in _L1_ffn_all.items() if k in ('g_info', 'W_qkv', 'W_proj', 'b_proj')}
    del _L1_ffn_all
    return {'x': x, 'L0_tok_W': _L0_tok_in['W'], 'L0_attn_Wq': _L0_attn_in['Wq'], 'L0_attn_Wk': _L0_attn_in['Wk'], 'L0_attn_Wv': _L0_attn_in['Wv'], 'L0_attn_Wo': _L0_attn_in['Wo'], 'L0_ffn_W_up': _L0_ffn_in['W_up'], 'L0_ffn_A_up': _L0_ffn_in['A_up'], 'L0_ffn_B_up': _L0_ffn_in['B_up'], 'L0_ffn_scale_up': _L0_ffn_in['scale_up'], 'L0_ffn_bias_up': _L0_ffn_in['bias_up'], 'L0_ffn_W_down': _L0_ffn_in['W_down'], 'L0_ffn_A_down': _L0_ffn_in['A_down'], 'L0_ffn_B_down': _L0_ffn_in['B_down'], 'L0_ffn_scale_down': _L0_ffn_in['scale_down'], 'L0_ffn_bias_down': _L0_ffn_in['bias_down'], 'L1_attn_Wq': _L1_attn_in['Wq'], 'L1_attn_Wk': _L1_attn_in['Wk'], 'L1_attn_Wv': _L1_attn_in['Wv'], 'L1_attn_Wo': _L1_attn_in['Wo'], 'L1_ffn_g_info': _L1_ffn_in['g_info'], 'L1_ffn_W_qkv': _L1_ffn_in['W_qkv'], 'L1_ffn_W_proj': _L1_ffn_in['W_proj'], 'L1_ffn_b_proj': _L1_ffn_in['b_proj']}

def reference(x, L0_tok_W, L0_attn_Wq, L0_attn_Wk, L0_attn_Wv, L0_attn_Wo, L0_ffn_W_up, L0_ffn_A_up, L0_ffn_B_up, L0_ffn_scale_up, L0_ffn_bias_up, L0_ffn_W_down, L0_ffn_A_down, L0_ffn_B_down, L0_ffn_scale_down, L0_ffn_bias_down, L1_attn_Wq, L1_attn_Wk, L1_attn_Wv, L1_attn_Wo, L1_ffn_g_info, L1_ffn_W_qkv, L1_ffn_W_proj, L1_ffn_b_proj):
    import jax
    import jax.numpy as jnp

    def _L0_tok_ref(input, W):
        import jax, jax.numpy as jnp
        import numpy as np
        VOCAB = 50257
        D_MODEL = 256
        BATCH = 4
        SEQ = 1024
        return jnp.take(W.T, input, axis=0)

    def _L0_attn_ref(x, Wq, Wk, Wv, Wo):
        import jax, jax.numpy as jnp
        import numpy as np
        THETA = 10000.0

        def _rope(x, pos):
            hd = x.shape[-1]
            inv_freq = 1.0 / THETA ** (jnp.arange(0, hd, 2, dtype=jnp.float32) / hd)
            ang = pos.astype(jnp.float32)[:, None] * inv_freq[None, :]
            cos, sin = (jnp.cos(ang), jnp.sin(ang))
            x1, x2 = (x[..., 0::2], x[..., 1::2])
            r1 = x1 * cos - x2 * sin
            r2 = x1 * sin + x2 * cos
            return jnp.stack([r1, r2], axis=-1).reshape(x.shape)
        b, s, d = x.shape
        n_heads = 16
        hd = d // n_heads

        def split_heads(t):
            return t.reshape(b, s, n_heads, hd).transpose(0, 2, 1, 3)
        q = split_heads(x @ Wq.T)
        k = split_heads(x @ Wk.T)
        v = split_heads(x @ Wv.T)
        pos = jnp.arange(s)
        q = _rope(q, pos)
        k = _rope(k, pos)
        scores = jnp.einsum('bhqd,bhkd->bhqk', q, k) / jnp.sqrt(jnp.float32(hd))
        causal = jnp.tril(jnp.ones((s, s), dtype=bool))
        scores = jnp.where(causal, scores, -jnp.inf)
        attn = jax.nn.softmax(scores, axis=-1)
        ctx = jnp.einsum('bhqk,bhkd->bhqd', attn, v)
        ctx = ctx.transpose(0, 2, 1, 3).reshape(b, s, d)
        return ctx @ Wo.T

    def _L0_ffn_ref(x, W_up, A_up, B_up, scale_up, bias_up, W_down, A_down, B_down, scale_down, bias_down):
        import jax, jax.numpy as jnp
        import numpy as np
        D_MODEL = 256
        D1, D2 = (32, 32)
        F1, F2 = (64, 64)
        E = 64
        TOP_K = 2

        def kmoe(x_flat, W_router, A, B, scale, bias, d_in1, d_in2, d_out1, d_out2, top_k):
            logits = x_flat @ W_router.T
            vals, idx = jax.lax.top_k(logits, top_k)
            probs = jax.nn.softmax(vals, axis=-1)
            xs = x_flat.reshape(-1, d_in1, d_in2)
            Ag = A[idx]
            Bg = B[idx]
            Y = jnp.einsum('nkoi,nij,nkpj->nkop', Ag, xs, Bg)
            out = jnp.einsum('nkop,nk->nop', Y, probs).reshape(-1, d_out1 * d_out2)
            return out * scale + bias
        orig_shape = x.shape
        x_flat = x.reshape(-1, D1 * D2)
        h = kmoe(x_flat, W_up, A_up, B_up, scale_up, bias_up, D1, D2, F1, F2, TOP_K)
        h = jax.nn.gelu(h, approximate=False)
        y = kmoe(h, W_down, A_down, B_down, scale_down, bias_down, F1, F2, D1, D2, TOP_K)
        return y.reshape(*orig_shape[:-1], D_MODEL)

    def _L1_attn_ref(x, Wq, Wk, Wv, Wo):
        import jax, jax.numpy as jnp
        import numpy as np
        D_MODEL = 256
        N_HEADS = 16
        HEAD_DIM = D_MODEL // N_HEADS
        ROPE_BASE = 10000.0

        def _rope_tables(T, dtype=jnp.float32):
            half = HEAD_DIM // 2
            inv_freq = 1.0 / ROPE_BASE ** (jnp.arange(0, HEAD_DIM, 2, dtype=jnp.float32) / HEAD_DIM)
            t = jnp.arange(T, dtype=jnp.float32)
            freqs = jnp.einsum('i,j->ij', t, inv_freq)
            return (jnp.cos(freqs).astype(dtype), jnp.sin(freqs).astype(dtype))

        def _apply_rotary(x, cos, sin):
            B, T, H, D = x.shape
            xr = x.reshape(B, T, H, D // 2, 2)
            x0, x1 = (xr[..., 0], xr[..., 1])
            c = cos[None, :, None, :]
            s = sin[None, :, None, :]
            out = jnp.stack([x0 * c - x1 * s, x0 * s + x1 * c], axis=-1)
            return out.reshape(B, T, H, D)
        B, T, C = x.shape
        H, Dh = (N_HEADS, HEAD_DIM)
        scale = Dh ** (-0.5)
        q = (x @ Wq.T).reshape(B, T, H, Dh)
        k = (x @ Wk.T).reshape(B, T, H, Dh)
        v = (x @ Wv.T).reshape(B, T, H, Dh)
        cos, sin = _rope_tables(T, x.dtype)
        q = _apply_rotary(q, cos, sin)
        k = _apply_rotary(k, cos, sin)
        q = q.transpose(0, 2, 1, 3).astype(jnp.float32)
        k = k.transpose(0, 2, 1, 3).astype(jnp.float32)
        v = v.transpose(0, 2, 1, 3)
        scores = jnp.einsum('bhqd,bhkd->bhqk', q, k) * scale
        causal = jnp.triu(jnp.ones((T, T), dtype=bool), k=1)
        scores = jnp.where(causal[None, None], -jnp.inf, scores)
        attn = jax.nn.softmax(scores, axis=-1).astype(v.dtype)
        out = jnp.einsum('bhqk,bhkd->bhqd', attn, v)
        out = out.transpose(0, 2, 1, 3).reshape(B, T, C)
        return out @ Wo.T

    def _L1_ffn_ref(x, g_info, W_qkv, W_proj, b_proj):
        import jax, jax.numpy as jnp
        import numpy as np
        B, N, C, H, REG = (1, 2309, 256, 16, 5)
        D = C // H
        Bx, Nx, Cx = x.shape
        scale = D ** (-0.5)
        qkv = (x @ W_qkv).reshape(Bx, Nx, 3, H, D)
        q, k, v = (qkv[:, :, 0], qkv[:, :, 1], qkv[:, :, 2])
        g_layer = g_info[0].reshape(-1, H, D)
        q_g = g_layer[0]
        q_pure = q[:, REG:]
        q_n = q_pure / jnp.linalg.norm(q_pure, axis=-1, keepdims=True)
        qg_n = q_g / jnp.linalg.norm(q_g, axis=-1, keepdims=True)
        sim = (qg_n[None, None] * q_n).sum(-1).mean(-1)
        sim = (sim - sim.min()) / (sim.max() - sim.min())
        pos = sim > 0.9
        logits = jnp.einsum('bqhd,bkhd->bhqk', q * scale, k)

        def masked_attn(tok_mask):
            key_mask = jnp.concatenate([jnp.ones((Bx, REG), bool), tok_mask], axis=1)
            l = jnp.where(key_mask[:, None, None, :], logits, -jnp.inf)
            a = jax.nn.softmax(l, axis=-1)
            return jnp.einsum('bhqk,bkhd->bqhd', a, v)
        x_pos = masked_attn(pos)
        x_neg = masked_attn(~pos)
        reg_out = (x_pos[:, :REG] + x_neg[:, :REG]) * 0.5
        tok_out = jnp.where(pos[:, :, None, None], x_pos[:, REG:], x_neg[:, REG:])
        out = jnp.concatenate([reg_out, tok_out], axis=1).reshape(Bx, Nx, Cx)
        return out @ W_proj + b_proj
    h = _L0_tok_ref(x, L0_tok_W)
    h = h + _L0_attn_ref(_layernorm(h, axis=-1), L0_attn_Wq, L0_attn_Wk, L0_attn_Wv, L0_attn_Wo)
    h = h + _L0_ffn_ref(_layernorm(h, axis=-1), L0_ffn_W_up, L0_ffn_A_up, L0_ffn_B_up, L0_ffn_scale_up, L0_ffn_bias_up, L0_ffn_W_down, L0_ffn_A_down, L0_ffn_B_down, L0_ffn_scale_down, L0_ffn_bias_down)
    h = h + _L1_attn_ref(_layernorm(h, axis=-1), L1_attn_Wq, L1_attn_Wk, L1_attn_Wv, L1_attn_Wo)
    h = h + _L1_ffn_ref(_layernorm(h, axis=-1), L1_ffn_g_info, L1_ffn_W_qkv, L1_ffn_W_proj, L1_ffn_b_proj)
    return h

_drawn_inputs = setup_inputs


def setup_inputs(seed=0):
    import zlib

    import numpy as np

    out = dict(_drawn_inputs(seed))
    spreads = {'L0_ffn_bias_up': (0.0, 0.8), 'L0_ffn_bias_down': (0.0, 0.1), 'L1_ffn_b_proj': (0.0, 0.1)}
    factors = {'L0_attn_Wq': 8.0,
     'L0_attn_Wk': 8.0,
     'L0_ffn_W_up': 8.0,
     'L0_ffn_A_up': 8.0,
     'L0_ffn_B_up': 8.0,
     'L0_ffn_W_down': 6.498,
     'L0_ffn_A_down': 6.005,
     'L0_ffn_B_down': 6.782,
     'L1_attn_Wq': 3.211,
     'L1_attn_Wk': 3.24,
     'L1_ffn_g_info': 8.0}
    for name, (base, spread) in spreads.items():
        noise = np.random.default_rng([zlib.crc32(name.encode()), seed]).standard_normal(out[name].shape)
        drawn = base * np.exp(spread * noise) if base else spread * noise
        out[name] = jnp.asarray(drawn.astype(out[name].dtype))
    for name, factor in factors.items():
        out[name] = (out[name] * factor).astype(out[name].dtype)
    return out
```

```python
from contextlib import ExitStack

import concourse.bass as bass
from concourse import mybir

F32 = mybir.dt.float32
BF16 = mybir.dt.bfloat16
I32 = mybir.dt.int32
U32 = mybir.dt.uint32
ALU = mybir.AluOpType
ACT = mybir.ActivationFunctionType
AX = mybir.AxisListType

P = 128
BATCH, SEQ, D = 2, 1024, 256
HEADS, HD = 16, 16
TOK = BATCH * SEQ
NT = TOK // P
TPB = SEQ // P
QK = 2 * D
COMPS = 6
KS = COMPS * HD
REG = 5
NEG = -1e30
SCALE = HD ** -0.5
EPS = 1e-5
E = 64
TOPK = 2
D1, F1 = 32, 64
SPM = D1 * D1 // D
NM = TOK // SPM
NMT = NM // P
GRP = 8
LAST = HD + 16

C_ID, C_MASK, C_MASKT, C_COS, C_SIN, C_REG, C_TOKM = 0, 128, 256, 384, 512, 640, 656
C_ONES, C_W = 688, 816


def scope(nc, ctx):
    def sb(name, shape, dt):
        return ctx.enter_context(nc.sbuf_tensor(name, shape, dt))

    def ps(name, shape, dt=F32):
        return ctx.enter_context(nc.psum_tensor(name, shape, dt))

    def sem(name):
        return ctx.enter_context(nc.semaphore(name))

    return sb, ps, sem


def part(i, n):
    return slice(i * n, (i + 1) * n) if isinstance(i, int) else bass.ds(i * n, n)


def at(i, n):
    return slice(i, i + n) if isinstance(i, int) else bass.ds(i, n)


def recycle(nc):
    ids = sorted(nc.released_uncleared_semaphores)
    start = 0
    for i in range(1, len(ids) + 1):
        if i == len(ids) or ids[i] != ids[i - 1] + 1:
            nc.sync.sem_clear(range(ids[start], ids[i - 1] + 1))
            start = i
    nc.all_engine_barrier()


def embed(nc, h, const, identb, KT, ids, rows_in, ids_dram, table, const_dram):
    with ExitStack() as ctx:
        sb, ps, sem = scope(nc, ctx)
        ids_in, const_in, made = sem("ids_in"), sem("const_in"), sem("made")
        block = ctx.enter_context(nc.Block())

        @block.sync
        def _(sp):
            sp.dma_start(ids[:, :], ids_dram).then_inc(ids_in, 16)
            sp.dma_start(const[:, :], const_dram).then_inc(const_in, 16)
            sp.wait_ge(const_in, 16)

        @block.vector
        def _(dve):
            nc.vector.memset(KT[KS:KS + 4, :], 1.0).then_inc(made, 1)
            dve.wait_ge(const_in, 16)
            nc.vector.tensor_copy(identb[:, :], const[:, C_ID:C_ID + P]).then_inc(made, 1)
            dve.wait_ge(made, 2)

        @block.gpsimd
        def _(pool):
            pool.wait_ge(ids_in, 16)
            for t in range(NT):
                nc.gpsimd.indirect_dma_start(
                    out=h[:, t * D:(t + 1) * D], out_offset=None, in_=table,
                    in_offset=bass.IndirectOffsetOnAxis(ap=ids[:, t:t + 1], axis=0)).then_inc(rows_in, 16)
            pool.wait_ge(rows_in, 16 * NT)


def statistics(nc, h, mean, rstd, name):
    with ExitStack() as ctx:
        sb, ps, sem = scope(nc, ctx)
        bn = sb(f"{name}_bn", [P, NT * 6], F32)
        mv = sb(f"{name}_mv", [P, NT * 2], F32)
        ve = sb(f"{name}_ve", [P, NT], F32)
        root = sb(f"{name}_root", [P, NT], F32)
        stats_done, var_done, root_done, newton = sem("stats_done"), sem("var_done"), sem("root_done"), sem("newton")
        mv3 = mv[:, :].rearrange("p (t c) -> p t c", c=2)
        block = ctx.enter_context(nc.Block())

        @block.vector
        def _(dve):
            with dve.Fori(0, NT) as t:
                nc.vector.bn_stats(bn[:, part(t, 6)], h[:, part(t, D)]).then_inc(stats_done, 1)
            dve.wait_ge(stats_done, NT)
            for t in range(NT):
                nc.vector.bn_aggr(mv[:, part(t, 2)], bn[:, part(t, 6)]).then_inc(stats_done, 1)
            dve.wait_ge(stats_done, 2 * NT)
            nc.vector.tensor_copy(mean[:, :], mv3[:, :, 0]).then_inc(newton, 1)
            nc.vector.tensor_scalar(ve[:, :], mv3[:, :, 1], EPS, None, ALU.add).then_inc(var_done, 1)
            dve.wait_ge(root_done, 1)
            nc.vector.reciprocal(rstd[:, :], root[:, :]).then_inc(newton, 1)
            dve.wait_ge(newton, 2)
            nc.vector.tensor_tensor(ve[:, :], ve[:, :], rstd[:, :], ALU.mult).then_inc(newton, 1)
            dve.wait_ge(newton, 3)
            nc.vector.tensor_tensor(ve[:, :], ve[:, :], root[:, :], ALU.add).then_inc(newton, 1)
            dve.wait_ge(newton, 4)
            nc.vector.tensor_scalar(ve[:, :], ve[:, :], 0.5, None, ALU.mult).then_inc(newton, 1)
            dve.wait_ge(newton, 5)
            nc.vector.reciprocal(rstd[:, :], ve[:, :]).then_inc(newton, 1)
            dve.wait_ge(newton, 6)

        @block.scalar
        def _(act):
            act.wait_ge(var_done, 1)
            nc.scalar.activation(root[:, :], ve[:, :], ACT.Sqrt).then_inc(root_done, 1)


def project(nc, h, mean, rstd, const, identb, w_qk_dram, w_v_dram, QT, KT, V, rope, name, gauge=None):
    with ExitStack() as ctx:
        sb, ps, sem = scope(nc, ctx)
        wqk = sb(f"{name}_wqk", [P, 2, QK], F32)
        wv = sb(f"{name}_wv", [P, 2, D], F32)
        xn = [sb(f"{name}_xn{i}", [P, D], F32) for i in range(1)]
        xT = sb(f"{name}_xT", [P, D], F32)
        turned = sb(f"{name}_turned", [P, QK], F32)
        cross = sb(f"{name}_cross", [P, QK], F32)
        rest = sb(f"{name}_rest", [P, QK], F32)
        hi = sb(f"{name}_hi", [P, QK], BF16)
        mid = sb(f"{name}_mid", [P, QK], BF16)
        stack = sb(f"{name}_stack", [P, 2, HEADS, KS], BF16)
        xT_ps = ps(f"{name}_xT_ps", [P, D])
        qk_ps = ps(f"{name}_qk_ps", [P, QK])
        v_ps = ps(f"{name}_v_ps", [P, D])
        st_ps = [ps(f"{name}_st_ps{j}", [P, 8 * P], BF16) for j in range(4)]
        w_in, xn_ready, xT_turned, xT_ready = sem("w_in"), sem("xn_ready"), sem("xT_turned"), sem("xT_ready")
        qkv_ready, v_used = sem("qkv_ready"), sem("v_used")
        turn_part, rot_ready, hi_ready, rest_ready, mid_ready = (
            sem("turn_part"), sem("rot_ready"), sem("hi_ready"), sem("rest_ready"), sem("mid_ready"))
        low_ready, stack_part, stack_turned, bank_used = (
            sem("low_ready"), sem("stack_part"), sem("stack_turned"), sem("bank_used"))
        bank_used_act = sem("bank_used_act")
        gauged = sem("gauged")
        ident = const[:, C_ID:C_ID + P]
        t3 = turned[:, :].rearrange("p (g i c) -> p g i c", g=2 * HEADS, c=2)
        if gauge is not None:
            gq, gdot, gnorm = gauge
            gtmp = sb(f"{name}_gtmp", [P, D], F32)
        block = ctx.enter_context(nc.Block())

        @block.sync
        def _(sp):
            sp.dma_start(wqk[:, :, :], w_qk_dram.rearrange("(c p) n -> p c n", p=P)).then_inc(w_in, 16)
            sp.dma_start(wv[:, :, :], w_v_dram.rearrange("(c p) n -> p c n", p=P)).then_inc(w_in, 16)
            sp.wait_ge(w_in, 32)

        @block.tensor
        def _(pe):
            def turn_x(t):
                pe.wait_ge(xn_ready, t + 1)
                for c in range(2):
                    mm = pe.transpose(xT_ps[:, c * P:(c + 1) * P], xn[0][:, c * P:(c + 1) * P], ident)
                mm.then_inc(xT_turned, 1)

            def products(t):
                pe.wait_ge(xT_ready, t + 1)
                pe.wait_ge(rot_ready, t)
                pe.wait_ge(v_used, t)
                for c in range(2):
                    pe.matmul(qk_ps[:, :], xT[:, c * P:(c + 1) * P], wqk[:, c, :], start=c == 0, stop=c == 1)
                for c in range(2):
                    mm = pe.matmul(v_ps[:, :], xT[:, c * P:(c + 1) * P], wv[:, c, :], start=c == 0, stop=c == 1)
                mm.then_inc(qkv_ready, 1)

            def turn_stack(t):
                pe.wait_ge(stack_part, 6 * t + 6)
                pe.wait_ge(low_ready, 2 * t + 2)
                pe.wait_ge(bank_used, 2 * t)
                pe.wait_ge(bank_used_act, 2 * t)
                for j in range(4):
                    for g in range(8):
                        mm = pe.transpose(st_ps[j][0:KS, g * P:(g + 1) * P],
                                          stack[:, j // 2, (j % 2) * 8 + g, :], identb[:, :])
                    mm.then_inc(stack_turned, 1)

            pe.wait_ge(w_in, 32)
            turn_x(0)
            products(0)
            with pe.Fori(1, NT) as t:
                turn_x(t)
                turn_stack(t - 1)
                products(t)
            turn_stack(NT - 1)

        @block.vector
        def _(dve):
            def norm(t):
                dve.wait_ge(xT_turned, t)
                nc.vector.tensor_scalar(xn[0][:, :], h[:, part(t, D)], mean[:, part(t, 1)],
                                        rstd[:, part(t, 1)], ALU.subtract, ALU.mult).then_inc(xn_ready, 1)

            def rotate(t, t_in_batch):
                dve.wait_ge(qkv_ready, t + 1)
                if rope:
                    cos = const[:, at(t_in_batch * HD + C_COS, HD)].unsqueeze(1).broadcast_to([P, 2 * HEADS, HD])
                    dve.wait_ge(low_ready, 2 * t)
                    nc.vector.tensor_tensor(turned[:, :].rearrange("p (g d) -> p g d", d=HD),
                                            qk_ps[:, :].rearrange("p (g d) -> p g d", d=HD),
                                            cos, ALU.mult).then_inc(turn_part, 1)
                    q4 = qk_ps[:, :].rearrange("p (g i c) -> p g i c", i=HD // 2, c=2)
                    c4 = cross[:, :].rearrange("p (g i c) -> p g i c", i=HD // 2, c=2)
                    for c in range(2):
                        sin = const[:, at(t_in_batch * HD + C_SIN, HD)].rearrange(
                            "p (i c) -> p i c", c=2)[:, :, c].unsqueeze(1).broadcast_to([P, 2 * HEADS, HD // 2])
                        nc.vector.tensor_tensor(c4[:, :, :, c], q4[:, :, :, 1 - c], sin, ALU.mult).then_inc(turn_part, 1)
                    dve.wait_ge(turn_part, 3 * t + 3)
                    nc.vector.tensor_tensor(turned[:, :], turned[:, :], cross[:, :], ALU.add).then_inc(rot_ready, 1)
                else:
                    dve.wait_ge(low_ready, 2 * t)
                    nc.vector.tensor_copy(turned[:, :], qk_ps[:, :]).then_inc(rot_ready, 1)
                    dve.wait_ge(rot_ready, t + 1)
                    nc.vector.tensor_tensor(gtmp[:, :], turned[:, 0:D], turned[:, 0:D], ALU.mult).then_inc(gauged, 1)
                    dve.wait_ge(gauged, 4 * t + 1)
                    nc.vector.tensor_reduce(gnorm[:, part(t, HEADS)],
                                            gtmp[:, :].rearrange("p (g d) -> p g d", d=HD), AX.X, ALU.add).then_inc(gauged, 1)
                    dve.wait_ge(gauged, 4 * t + 2)
                    nc.vector.tensor_tensor(gtmp[:, :], turned[:, 0:D], gq[:, :], ALU.mult).then_inc(gauged, 1)
                    dve.wait_ge(gauged, 4 * t + 3)
                    nc.vector.tensor_reduce(gdot[:, part(t, HEADS)],
                                            gtmp[:, :].rearrange("p (g d) -> p g d", d=HD), AX.X, ALU.add).then_inc(gauged, 1)
                    dve.wait_ge(gauged, 4 * t + 4)

            def assemble(t):
                s5 = stack[:, :, :, :].rearrange("p a g (c d) -> p a g c d", d=HD)
                h4 = hi[:, :].rearrange("p (a g d) -> p a g d", a=2, d=HD)
                m4 = mid[:, :].rearrange("p (a g d) -> p a g d", a=2, d=HD)
                dve.wait_ge(hi_ready, t + 1)
                dve.wait_ge(stack_turned, 4 * t)
                for a, lo in ((0, 0), (1, 2)):
                    nc.vector.tensor_copy(s5[:, a, :, lo:lo + 3, :],
                                          h4[:, a].unsqueeze(2).broadcast_to([P, HEADS, 3, HD])).then_inc(stack_part, 1)
                dve.wait_ge(mid_ready, t + 1)
                for a, cs in ((0, (3, 5)), (1, (0, 5))):
                    for c in cs:
                        nc.vector.tensor_copy(s5[:, a, :, c, :], m4[:, a]).then_inc(stack_part, 1)

            def copy_out(t):
                for j in range(2):
                    dve.wait_ge(stack_turned, 4 * t + j + 1)
                    nc.vector.tensor_copy(QT[0:KS, at(t * HEADS * P + j * 8 * P, 8 * P)],
                                          st_ps[j][0:KS, :]).then_inc(bank_used, 1)

            norm(0)
            for b in range(BATCH):
                with dve.Fori(0, TPB - 1) as tb:
                    norm(tb + (b * TPB + 1))
                    rotate(tb + b * TPB, tb)
                    assemble(tb + b * TPB)
                    copy_out(tb + b * TPB)
                if b == 0:
                    norm(TPB)
                rotate(b * TPB + TPB - 1, TPB - 1)
                assemble(b * TPB + TPB - 1)
                copy_out(b * TPB + TPB - 1)
            dve.wait_ge(bank_used, 2 * NT)

        @block.scalar
        def _(act):
            def copy_x(t):
                act.wait_ge(xT_turned, t + 1)
                act.wait_ge(qkv_ready, t)
                nc.scalar.copy(xT[:, :], xT_ps[:, :]).then_inc(xT_ready, 1)

            def split(t):
                act.wait_ge(qkv_ready, t + 1)
                nc.scalar.copy(V[:, part(t, D)], v_ps[:, :]).then_inc(v_used, 1)
                act.wait_ge(rot_ready, t + 1)
                act.wait_ge(stack_part, 6 * t)
                nc.scalar.copy(hi[:, :], turned[:, :]).then_inc(hi_ready, 1)
                act.wait_ge(rest_ready, t + 1)
                act.wait_ge(low_ready, 2 * t)
                nc.scalar.copy(mid[:, :], rest[:, :]).then_inc(mid_ready, 1)

            def copy_out(t):
                for j in range(2):
                    act.wait_ge(stack_turned, 4 * t + j + 3)
                    nc.scalar.copy(KT[0:KS, at(t * HEADS * P + j * 8 * P, 8 * P)],
                                   st_ps[2 + j][0:KS, :]).then_inc(bank_used_act, 1)

            copy_x(0)
            split(0)
            with act.Fori(1, NT) as t:
                copy_x(t)
                copy_out(t - 1)
                split(t)
            copy_out(NT - 1)
            act.wait_ge(bank_used_act, 2 * NT)

        @block.gpsimd
        def _(pool):
            with pool.Fori(0, NT) as t:
                pool.wait_ge(hi_ready, t + 1)
                pool.wait_ge(mid_ready, t)
                nc.gpsimd.tensor_tensor(rest[:, :], turned[:, :], hi[:, :], ALU.subtract).then_inc(rest_ready, 1)
                pool.wait_ge(mid_ready, t + 1)
                pool.wait_ge(stack_turned, 4 * t)
                s5 = stack[:, :, :, :].rearrange("p a g (c d) -> p a g c d", d=HD)
                r4 = rest[:, :].rearrange("p (a g d) -> p a g d", a=2, d=HD)
                m4 = mid[:, :].rearrange("p (a g d) -> p a g d", a=2, d=HD)
                for a, c in ((0, 4), (1, 1)):
                    nc.gpsimd.tensor_tensor(s5[:, a, :, c, :], r4[:, a], m4[:, a], ALU.subtract).then_inc(low_ready, 1)


def attend(nc, const, identb, QT, KT, V, ctx_out, causal, name, extra=None):
    with ExitStack() as ctx:
        sb, ps, sem = scope(nc, ctx)
        CHUNKS = [(qt, c) for qt in range(TPB) for c in range((qt if causal else TPB - 1) // 4 + 1)]
        NCH = len(CHUNKS)
        KM = KS + (0 if causal else 2)
        KE = KM + 2
        USES = NCH + 2
        assert USES % 2 == 0
        maskb = sb(f"{name}_maskb", [P, 2 * P], BF16)
        vst = sb(f"{name}_vst", [P, TPB, 32], F32)
        probs = [sb(f"{name}_probs{i}", [P, SEQ], F32) for i in range(2)]
        mxp = sb(f"{name}_mxp", [P, 2, TPB], F32)
        mx = sb(f"{name}_mx", [P, TPB], F32)
        negm = sb(f"{name}_negm", [P, TPB, KE], BF16)
        oT = sb(f"{name}_oT", [P, 2 * P], F32)
        rec = sb(f"{name}_rec", [P, TPB], F32)
        small = [ps(f"{name}_small{i}", [P, 512]) for i in range(2)]
        wide = [ps(f"{name}_wide{i}", [P, SEQ]) for i in range(2)]
        out_ps = [ps(f"{name}_out{i}", [P, 512]) for i in range(2)]
        consts_set = sem("consts_set")
        small_filled = [sem("small_filled0"), sem("small_filled1")]
        small_used = [sem("small_used0"), sem("small_used1")]
        scores_ready = [sem("scores_ready0"), sem("scores_ready1")]
        probs_ready = [sem("probs_ready0"), sem("probs_ready1")]
        probs_used = [sem("probs_used0"), sem("probs_used1")]
        max_part, mx_ready, hi_set, negm_ready, rows_ready = (
            sem("max_part"), sem("mx_ready"), sem("hi_set"), sem("negm_ready"), sem("rows_ready"))
        v_staged, oT_ready, rec_ready, head_done = sem("v_staged"), sem("oT_ready"), sem("rec_ready"), sem("head_done")
        ones_set, pen_set, oT_part = sem("ones_set"), sem("pen_set"), sem("oT_part")
        if extra is not None:
            QX, ctx_x, pen = extra
            probs_x = sb(f"{name}_probs_x", [P, TPB * REG], F32)
            oT_x = sb(f"{name}_oT_x", [32, REG], F32)
            rec_x = sb(f"{name}_rec_x", [REG, 1], F32)
            xscores_ready, xprobs_ready, xout_ready = sem("xscores_ready"), sem("xprobs_ready"), sem("xout_ready")
            XS, XO = P, P
        ident = const[:, C_ID:C_ID + P]
        block = ctx.enter_context(nc.Block())

        def use(b, k, r):
            return k % 2, r * (USES // 2) + (b * HEADS * (USES // 2) + k // 2)

        def chunk_use(b, j, r, first):
            return use(b, j, 0) if first else use(b, NCH + 1 + j, r)

        def end_use(b, r, last):
            return use(b, NCH + 1 + (0 if last else NCH + 1), r)

        def tile_of(M, rows, b, r, t):
            return M[rows, at(r * P + (b * TPB + t) * HEADS * P, P)]

        def tiles_of(M, rows, b, r, t0, n):
            m3 = M[rows, (b * TPB + t0) * HEADS * P:(b * TPB + t0 + n) * HEADS * P].rearrange(
                "p (t x) -> p t x", t=n)
            return m3[:, :, at(r * P, P)]

        def num(b, r):
            return r + b * HEADS

        def per_head(eng, body):
            def run(b):
                with eng.Fori(0, HEADS - 1) as r:
                    body(b, r, False)
                body(b, HEADS - 1, True)
            return run

        @block.tensor
        def _(pe):
            def max_scores(b, r, j, first):
                qt, c = CHUNKS[j]
                nxt = 0 if first else r + 1
                bank, before = chunk_use(b, j, r, first)
                tiles = min(4, qt + 1 - 4 * c) if causal else 4
                diag = causal and qt // 4 == c
                pe.wait_ge(small_used[bank], before)
                out = small[bank][:, 0:tiles * P].rearrange("p (t x) -> p t x", t=tiles)
                mm = pe.matmul(out, tile_of(QT, slice(0, KM), b, nxt, qt),
                               tiles_of(KT, slice(0, KM), b, nxt, 4 * c, tiles), start=True, stop=not diag)
                if diag:
                    mm = pe.matmul(small[bank][:, (tiles - 1) * P:tiles * P], identb[:, :], maskb[:, 0:P],
                                   start=False, stop=True)
                mm.then_inc(small_filled[bank], 1)

            def turn_max(b, r, first):
                bank, before = chunk_use(b, NCH, r, first)
                pe.wait_ge(negm_ready, num(b, 0 if first else r + 1) + 1)
                pe.wait_ge(small_used[bank], before)
                rows = small[bank][:, :].bitcast(BF16)
                for t in range(TPB):
                    mm = pe.transpose(rows[0:KE, t * P:(t + 1) * P], negm[:, t, :], identb[:, :])
                mm.then_inc(small_filled[bank], 1)

            def exp_scores(b, r, kb):
                w, n = kb % 2, num(b, r)
                first_q = kb if causal else 0
                if kb == 0:
                    pe.wait_ge(rows_ready, n + 1)
                pe.wait_ge(probs_ready[w], n * (TPB // 2) + kb // 2)
                for q0 in range(first_q, TPB, 4):
                    tiles = min(4, TPB - q0)
                    col = (q0 - first_q) * P
                    diag = causal and q0 == kb
                    mm = pe.matmul(wide[w][:, col:col + tiles * P].rearrange("p (t x) -> p t x", t=tiles),
                                   tile_of(KT, slice(0, KE), b, r, kb),
                                   tiles_of(QT, slice(0, KE), b, r, q0, tiles), start=True, stop=not diag)
                    if diag:
                        mm = pe.matmul(wide[w][:, 0:P], identb[:, :], maskb[:, P:2 * P], start=False, stop=True)
                mm.then_inc(scores_ready[w], 1)

            def values(b, r, kb):
                w, n = kb % 2, num(b, r)
                if kb == 0:
                    pe.wait_ge(v_staged, n + 1)
                    pe.wait_ge(oT_ready, n)
                    if extra is not None:
                        pe.wait_ge(xprobs_ready, n + 1)
                pe.wait_ge(probs_ready[w], n * (TPB // 2) + kb // 2 + 1)
                first_q = kb if causal else 0
                for qt in range(first_q, TPB):
                    g = qt % 4
                    mm = pe.matmul(out_ps[qt // 4][32 * g:32 * g + 32, 0:P], vst[:, kb, :],
                                   probs[w][:, (qt - first_q) * P:(qt - first_q + 1) * P],
                                   start=kb == 0, stop=kb == (qt if causal else TPB - 1))
                mm.then_inc(probs_used[w], 1)

            def extra_scores(b, r):
                n = num(b, r)
                pe.wait_ge(rows_ready, n + 1)
                pe.wait_ge(xprobs_ready, n)
                pe.wait_ge(oT_ready, n)
                for kb in range(TPB):
                    mm = pe.matmul(out_ps[1][:, XS + kb * REG:XS + (kb + 1) * REG],
                                   tile_of(KT, slice(0, KE), b, r, kb), QX[0:KE, part(n, REG)],
                                   start=True, stop=True)
                mm.then_inc(xscores_ready, 1)

            def extra_values(b, r):
                pe.wait_ge(xprobs_ready, num(b, r) + 1)
                for kb in range(TPB):
                    mm = pe.matmul(out_ps[0][0:32, XO:XO + REG], vst[:, kb, :],
                                   probs_x[:, kb * REG:(kb + 1) * REG], start=kb == 0, stop=kb == TPB - 1)
                mm.then_inc(xout_ready, 1)

            def turn_out(b, r, last):
                bank, before = end_use(b, r, last)
                pe.wait_ge(oT_ready, num(b, r) + 1)
                pe.wait_ge(small_used[bank], before)
                for c in range(2):
                    mm = pe.transpose(small[bank][:, c * P:(c + 1) * P], oT[:, c * P:(c + 1) * P], ident)
                if extra is not None:
                    mm = pe.transpose(small[bank][0:REG, 2 * P:2 * P + 32], oT_x[:, :],
                                      const[0:32, C_ID:C_ID + 32])
                mm.then_inc(small_filled[bank], 1)

            def head(b, r, last):
                done = 0
                if extra is not None:
                    extra_scores(b, r)
                for kb in range(TPB):
                    upto = NCH * (kb + 1) // TPB if not causal else min(NCH, 2 * (kb + 1), kb + 5)
                    while not last and done < upto:
                        max_scores(b, r, done, False)
                        done += 1
                    exp_scores(b, r, kb)
                    if kb >= 1:
                        values(b, r, kb - 1)
                assert last or done == NCH
                values(b, r, TPB - 1)
                if extra is not None:
                    extra_values(b, r)
                if not last:
                    turn_max(b, r, False)
                turn_out(b, r, last)

            pe.wait_ge(consts_set, 4)
            run = per_head(pe, head)
            for b in range(BATCH):
                for j in range(NCH):
                    max_scores(b, 0, j, True)
                turn_max(b, 0, True)
                run(b)

        @block.vector
        def _(dve):
            def maxima(b, r, first):
                n = num(b, 0 if first else r + 1)
                for j, (qt, c) in enumerate(CHUNKS):
                    bank, before = chunk_use(b, j, r, first)
                    tiles = min(4, qt + 1 - 4 * c) if causal else 4
                    dve.wait_ge(small_filled[bank], before + 1)
                    nc.vector.tensor_reduce(mxp[:, c, qt:qt + 1], small[bank][:, 0:tiles * P], AX.X,
                                            ALU.max).then_inc(small_used[bank], 1)
                for j in (NCH - 2, NCH - 1):
                    bank, before = chunk_use(b, j, r, first)
                    dve.wait_ge(small_used[bank], before + 1)
                nc.vector.tensor_tensor(mx[:, :], mxp[:, 0, :], mxp[:, 1, :], ALU.max).then_inc(mx_ready, 1)
                dve.wait_ge(mx_ready, n + 1)
                dve.wait_ge(rows_ready, n)
                nc.vector.tensor_scalar(negm[:, :, KM], mx[:, :], -1.0, None, ALU.mult).then_inc(hi_set, 1)
                dve.wait_ge(hi_set, n + 1)
                nc.vector.scalar_tensor_tensor(negm[:, :, KM + 1], mx[:, :], -1.0, negm[:, :, KM],
                                               ALU.mult, ALU.subtract).then_inc(negm_ready, 1)

            def divide(b, r, last):
                n = num(b, r)
                bank, before = end_use(b, r, last)
                rows = small[bank][:, 0:2 * P].rearrange("p (t x) -> p t x", x=32)
                if last:
                    bank_before, before_that = end_use(b, r - 1, False)
                    dve.wait_ge(small_used[bank_before], before_that + 1)
                dve.wait_ge(small_filled[bank], before + 1)
                nc.vector.reciprocal(rec[:, :].unsqueeze(2), rows[:, :, HD:HD + 1]).then_inc(rec_ready, 1)
                if extra is not None:
                    nc.vector.reciprocal(rec_x[:, :], small[bank][0:REG, 2 * P + HD:2 * P + HD + 1]).then_inc(rec_ready, 1)
                dve.wait_ge(rec_ready, (n + 1) * (1 if extra is None else 2))
                if extra is not None:
                    nc.vector.tensor_scalar(ctx_x[:, part(n, HD)], small[bank][0:REG, 2 * P:2 * P + HD],
                                            rec_x[:, 0:1], None, ALU.mult).then_inc(head_done, 1)
                dst = ctx_out[:, b * TPB * D:(b + 1) * TPB * D].rearrange("p (t x) -> p t x", t=TPB)
                nc.vector.tensor_tensor(dst[:, :, at(r * HD, HD)], rows[:, :, 0:HD],
                                        rec[:, :].unsqueeze(2).broadcast_to([P, TPB, HD]),
                                        ALU.mult).then_inc(small_used[bank], 1)

            def head(b, r, last):
                if not last:
                    maxima(b, r, False)
                divide(b, r, last)

            nc.vector.tensor_copy(maskb[:, :], const[:, C_MASK:C_MASK + 2 * P]).then_inc(consts_set, 1)
            nc.vector.memset(mxp[:, :, :], -3e38).then_inc(consts_set, 1)
            nc.vector.memset(negm[:, :, :], 0.0).then_inc(consts_set, 1)
            nc.vector.memset(vst[:, :, :], 0.0).then_inc(consts_set, 1)
            dve.wait_ge(consts_set, 4)
            nc.vector.memset(vst[:, :, HD:HD + 1], 1.0).then_inc(ones_set, 1)
            run = per_head(dve, head)
            for b in range(BATCH):
                if extra is not None:
                    dve.wait_ge(rows_ready, b * HEADS)
                    nc.vector.tensor_copy(negm[:, :, KS:KS + 2], pen[:, b * TPB * 2:(b + 1) * TPB * 2].rearrange(
                        "p (t c) -> p t c", c=2)).then_inc(pen_set, 1)
                maxima(b, 0, True)
                run(b)
            for bank in range(2):
                dve.wait_ge(small_used[bank], BATCH * HEADS * (USES // 2))

        @block.scalar
        def _(act):
            def rows(b, r, first):
                bank, before = chunk_use(b, NCH, r, first)
                act.wait_ge(small_filled[bank], before + 1)
                nxt = 0 if first else r + 1
                src = small[bank][:, :].bitcast(BF16)[KS:KE, :].rearrange("p (t x) -> p t x", t=TPB)
                nc.scalar.copy(tiles_of(QT, slice(KS, KE), b, nxt, 0, TPB), src).then_inc(rows_ready, 1)
                act.wait_ge(rows_ready, num(b, nxt) + 1)
                act.sem_inc(small_used[bank], 1)

            def head(b, r, last):
                n = num(b, r)
                if extra is not None:
                    act.wait_ge(xscores_ready, n + 1)
                    act.wait_ge(xout_ready, n)
                    nc.scalar.activation(probs_x[:, :], out_ps[1][:, XS:XS + TPB * REG], ACT.Exp,
                                         scale=SCALE).then_inc(xprobs_ready, 1)
                for kb in range(TPB):
                    w = kb % 2
                    cols = (TPB - kb if causal else TPB) * P
                    act.wait_ge(scores_ready[w], n * (TPB // 2) + kb // 2 + 1)
                    act.wait_ge(probs_used[w], n * (TPB // 2) + kb // 2)
                    nc.scalar.activation(probs[w][:, 0:cols], wide[w][:, 0:cols], ACT.Exp,
                                         scale=SCALE).then_inc(probs_ready[w], 1)
                act.wait_ge(probs_used[1], (n + 1) * (TPB // 2))
                act.wait_ge(rec_ready, n * (1 if extra is None else 2))
                if extra is not None:
                    act.wait_ge(xout_ready, n + 1)
                nc.scalar.copy(oT[:, 0:P], out_ps[0][:, 0:P]).then_inc(oT_part, 1)
                if extra is not None:
                    nc.scalar.copy(oT_x[:, :], out_ps[0][0:32, XO:XO + REG]).then_inc(oT_part, 1)
                act.wait_ge(oT_part, (n + 1) * (1 if extra is None else 2))
                nc.scalar.copy(oT[:, P:2 * P], out_ps[1][:, 0:P]).then_inc(oT_ready, 1)
                if not last:
                    rows(b, r, False)

            run = per_head(act, head)
            for b in range(BATCH):
                rows(b, 0, True)
                run(b)

        @block.gpsimd
        def _(pool):
            pool.wait_ge(ones_set, 1)
            for b in range(BATCH):
                with pool.Fori(0, HEADS) as r:
                    n = num(b, r)
                    pool.wait_ge(probs_used[1], n * (TPB // 2))
                    if extra is not None:
                        pool.wait_ge(xout_ready, n)
                    src = V[:, b * TPB * D:(b + 1) * TPB * D].rearrange("p (t x) -> p t x", t=TPB)
                    nc.gpsimd.tensor_copy(vst[:, :, 0:HD], src[:, :, at(r * HD, HD)]).then_inc(v_staged, 1)


def project_out(nc, h, ctx_in, const, w_dram, name, bias_dram=None, out_dram=None):
    with ExitStack() as ctx:
        sb, ps, sem = scope(nc, ctx)
        w = sb(f"{name}_w", [P, 2, D], F32)
        stage = [sb(f"{name}_stage{i}", [P, D], F32) for i in range(2)]
        cT = [sb(f"{name}_cT{i}", [P, D], F32) for i in range(2)]
        cT_ps = [ps(f"{name}_cT_ps{i}", [P, D]) for i in range(2)]
        y_ps = [ps(f"{name}_y_ps{i}", [P, D]) for i in range(2)]
        w_in = sem("w_in")
        staged = [sem("staged0"), sem("staged1")]
        turned = [sem("turned0"), sem("turned1")]
        cT_ready = [sem("cT_ready0"), sem("cT_ready1")]
        y_ready = [sem("y_ready0"), sem("y_ready1")]
        added = [sem("added0"), sem("added1")]
        stored = sem("stored")
        NW = 16
        if bias_dram is not None:
            bias = sb(f"{name}_bias", [1, D], F32)
            NW = 32
        ident = const[:, C_ID:C_ID + P]
        block = ctx.enter_context(nc.Block())

        @block.sync
        def _(sp):
            sp.dma_start(w[:, :, :], w_dram.rearrange("(c p) n -> p c n", p=P)).then_inc(w_in, 16)
            if bias_dram is not None:
                sp.dma_start(bias[:, :], bias_dram.rearrange("(a n) -> a n", a=1)).then_inc(w_in, 16)
            if out_dram is not None:
                o3 = out_dram.rearrange("b (t p) d -> p (b t) d", p=P)
                h3 = h[:, :].rearrange("p (t d) -> p t d", d=D)
                for c in range(4):
                    for i in range(2):
                        sp.wait_ge(added[i], 2 * (c + 1))
                    sp.dma_start(o3[:, 4 * c:4 * c + 4, :], h3[:, 4 * c:4 * c + 4, :]).then_inc(stored, 16)
                sp.wait_ge(stored, 64)

        @block.gpsimd
        def _(pool):
            with pool.Fori(0, NT // 2) as s:
                for i in range(2):
                    pool.wait_ge(turned[i], s)
                    nc.gpsimd.tensor_copy(stage[i][:, :], ctx_in[:, at(s * 2 * D + i * D, D)]).then_inc(staged[i], 1)

        @block.tensor
        def _(pe):
            pe.wait_ge(w_in, NW)
            with pe.Fori(0, NT // 2) as s:
                for i in range(2):
                    pe.wait_ge(staged[i], s + 1)
                    pe.wait_ge(cT_ready[i], s)
                    for c in range(2):
                        mm = pe.transpose(cT_ps[i][:, c * P:(c + 1) * P], stage[i][:, c * P:(c + 1) * P], ident)
                    mm.then_inc(turned[i], 1)
                for i in range(2):
                    pe.wait_ge(cT_ready[i], s + 1)
                    pe.wait_ge(added[i], s)
                    for c in range(2):
                        mm = pe.matmul(y_ps[i][:, :], cT[i][:, c * P:(c + 1) * P], w[:, c, :],
                                       start=c == 0, stop=c == 1 and bias_dram is None)
                    if bias_dram is not None:
                        mm = pe.matmul(y_ps[i][:, :], const[0:1, C_ONES:C_ONES + P], bias[:, :], start=False, stop=True)
                    mm.then_inc(y_ready[i], 1)

        @block.scalar
        def _(act):
            with act.Fori(0, NT // 2) as s:
                for i in range(2):
                    act.wait_ge(turned[i], s + 1)
                    act.wait_ge(y_ready[i], s)
                    nc.scalar.copy(cT[i][:, :], cT_ps[i][:, :]).then_inc(cT_ready[i], 1)

        @block.vector
        def _(dve):
            with dve.Fori(0, NT // 2) as s:
                for i in range(2):
                    dve.wait_ge(y_ready[i], s + 1)
                    hs = h[:, at(s * 2 * D + i * D, D)]
                    nc.vector.tensor_tensor(hs, y_ps[i][:, :], hs, ALU.add).then_inc(added[i], 1)
            for i in range(2):
                dve.wait_ge(added[i], NT // 2)


def set_ones(nc, KT):
    with ExitStack() as ctx:
        sb, ps, sem = scope(nc, ctx)
        made = sem("made")
        block = ctx.enter_context(nc.Block())

        @block.vector
        def _(dve):
            nc.vector.memset(KT[KS:KS + 4, :], 1.0).then_inc(made, 1)
            dve.wait_ge(made, 1)


def refined_root(dve, nc, root, x, tmp, done, base):
    nc.vector.reciprocal(tmp, root).then_inc(done, 1)
    dve.wait_ge(done, base + 1)
    nc.vector.tensor_tensor(tmp, tmp, x, ALU.mult).then_inc(done, 1)
    dve.wait_ge(done, base + 2)
    nc.vector.tensor_tensor(tmp, tmp, root, ALU.add).then_inc(done, 1)
    dve.wait_ge(done, base + 3)
    nc.vector.tensor_scalar(root, tmp, 0.5, None, ALU.mult).then_inc(done, 1)
    dve.wait_ge(done, base + 4)


def gauge_vector(nc, gq, g_dram):
    with ExitStack() as ctx:
        sb, ps, sem = scope(nc, ctx)
        sq = sb("gv_sq", [P, D], F32)
        n2 = sb("gv_n2", [P, HEADS], F32)
        root = sb("gv_root", [P, HEADS], F32)
        tmp = sb("gv_tmp", [P, HEADS], F32)
        g_in, step, n2_ready, root_ready = sem("g_in"), sem("step"), sem("n2_ready"), sem("root_ready")
        block = ctx.enter_context(nc.Block())

        @block.sync
        def _(sp):
            sp.dma_start(gq[:, :], g_dram[0, 0:1, :].broadcast_to([P, D])).then_inc(g_in, 16)
            sp.wait_ge(g_in, 16)

        @block.vector
        def _(dve):
            g3 = gq[:, :].rearrange("p (g d) -> p g d", d=HD)
            dve.wait_ge(g_in, 16)
            nc.vector.tensor_tensor(sq[:, :], gq[:, :], gq[:, :], ALU.mult).then_inc(step, 1)
            dve.wait_ge(step, 1)
            nc.vector.tensor_reduce(n2[:, :], sq[:, :].rearrange("p (g d) -> p g d", d=HD), AX.X,
                                    ALU.add).then_inc(n2_ready, 1)
            dve.wait_ge(root_ready, 1)
            refined_root(dve, nc, root[:, :], n2[:, :], tmp[:, :], step, 1)
            nc.vector.reciprocal(tmp[:, :], root[:, :]).then_inc(step, 1)
            dve.wait_ge(step, 6)
            nc.vector.tensor_tensor(g3, g3, tmp[:, :].unsqueeze(2).broadcast_to([P, HEADS, HD]),
                                    ALU.mult).then_inc(step, 1)
            dve.wait_ge(step, 7)

        @block.scalar
        def _(act):
            act.wait_ge(n2_ready, 1)
            nc.scalar.activation(root[:, :], n2[:, :], ACT.Sqrt).then_inc(root_ready, 1)


def group_tokens(nc, const, identb, gdot, gnorm, QT, KT, QX, pen):
    with ExitStack() as ctx:
        sb, ps, sem = scope(nc, ctx)
        NTH = NT * HEADS
        KM, KE = KS + 2, KS + 4
        RX = HEADS * REG
        root = sb("gt_root", [P, NTH], F32)
        tmp = sb("gt_tmp", [P, NTH], F32)
        sim = sb("gt_sim", [P, NT], F32)
        ends = sb("gt_ends", [P, 2, NT], F32)
        end1 = sb("gt_end1", [P, 2], F32)
        endall = sb("gt_endall", [P, 2], F32)
        width = sb("gt_width", [P, 2], F32)
        flag = sb("gt_flag", [P, NT], F32)
        qflag = sb("gt_qflag", [P, NT], F32)
        rows = sb("gt_rows", [P, 2, NT, KE], BF16)
        rowT = sb("gt_rowT", [KE, 2, NT * P], BF16)
        QZ = sb("gt_QZ", [KM, HEADS * (RX + REG)], BF16)
        zx = sb("gt_zx", [RX, BATCH, KE], BF16)
        mxx = sb("gt_mxx", [RX, BATCH], F32)
        row_ps = [ps(f"gt_row_ps{i}", [KE, TPB * P], BF16) for i in range(4)]
        x_ps = ps("gt_x_ps", [RX, SEQ])
        zx_ps = ps("gt_zx_ps", [KE, BATCH * RX], BF16)
        step, root_ready, ends_ready, ends_all, flags_ready = (
            sem("step"), sem("root_ready"), sem("ends_ready"), sem("ends_all"), sem("flags_ready"))
        rows_turned, rowT_ready, spread, zero, qz_ready, x_ready, zx_ready, zx_turned = (
            sem("rows_turned"), sem("rowT_ready"), sem("spread"), sem("zero"), sem("qz_ready"), sem("x_ready"),
            sem("zx_ready"), sem("zx_turned"))
        token = const[:, C_TOKM:C_TOKM + NT]
        block = ctx.enter_context(nc.Block())

        @block.scalar
        def _(act):
            nc.scalar.activation(root[:, :], gnorm[:, :], ACT.Sqrt).then_inc(root_ready, 1)
            for i in range(4):
                act.wait_ge(rows_turned, i + 1)
                nc.scalar.copy(rowT[KS:KS + 2, i // 2, (i % 2) * TPB * P:(i % 2 + 1) * TPB * P],
                               row_ps[i][KS:KS + 2, :]).then_inc(rowT_ready, 1)

        @block.vector
        def _(dve):
            n = 0

            def then(ins):
                nonlocal n
                n += 1
                ins.then_inc(step, 1)
                dve.wait_ge(step, n)

            nc.vector.memset(rows[:, :, :, :], 0.0).then_inc(zero, 1)
            nc.vector.memset(QZ[:, :], 0.0).then_inc(zero, 1)
            nc.vector.memset(zx[:, :, :], 0.0).then_inc(zero, 1)
            dve.wait_ge(root_ready, 1)
            refined_root(dve, nc, root[:, :], gnorm[:, :], tmp[:, :], step, 0)
            n = 4
            then(nc.vector.reciprocal(tmp[:, :], root[:, :]))
            then(nc.vector.tensor_tensor(tmp[:, :], gdot[:, :], tmp[:, :], ALU.mult))
            then(nc.vector.tensor_reduce(sim[:, :], tmp[:, :].rearrange("p (t g) -> p t g", g=HEADS), AX.X, ALU.add))
            then(nc.vector.tensor_scalar(sim[:, :], sim[:, :], 1.0 / HEADS, None, ALU.mult))
            then(nc.vector.tensor_tensor(ends[:, 0, :], sim[:, :], const[:, C_REG:C_REG + NT], ALU.add))
            then(nc.vector.scalar_tensor_tensor(ends[:, 1, :], sim[:, :], -1.0, const[:, C_REG:C_REG + NT],
                                                ALU.mult, ALU.add))
            nc.vector.tensor_reduce(end1[:, :], ends[:, :, :], AX.X, ALU.max).then_inc(ends_ready, 1)
            dve.wait_ge(ends_all, 1)
            then(nc.vector.tensor_tensor(width[:, 0:1], endall[:, 0:1], endall[:, 1:2], ALU.add))
            then(nc.vector.reciprocal(width[:, 1:2], width[:, 0:1]))
            then(nc.vector.tensor_scalar(sim[:, :], sim[:, :], endall[:, 1:2], width[:, 1:2], ALU.add, ALU.mult))
            then(nc.vector.tensor_scalar(flag[:, :], sim[:, :], 0.9, None, ALU.is_gt))
            dve.wait_ge(zero, 3)
            then(nc.vector.tensor_tensor(flag[:, :], flag[:, :], token, ALU.mult))
            then(nc.vector.tensor_copy(rows[:, 0, :, KS], flag[:, :]))
            then(nc.vector.tensor_tensor(rows[:, 0, :, KS + 1], token, flag[:, :], ALU.subtract))
            then(nc.vector.tensor_tensor(qflag[:, :], flag[:, :], token, ALU.subtract))
            then(nc.vector.tensor_scalar(qflag[:, :], qflag[:, :], 1.0, None, ALU.add))
            p3 = pen[:, :].rearrange("p (t c) -> p t c", c=2)
            then(nc.vector.tensor_scalar(p3[:, :, 0], qflag[:, :], -NEG, NEG, ALU.mult, ALU.add))
            then(nc.vector.tensor_scalar(p3[:, :, 1], qflag[:, :], NEG, None, ALU.mult))
            nc.vector.tensor_copy(rows[:, 1, :, KS:KS + 2], p3).then_inc(flags_ready, 1)
            for b in range(BATCH):
                src = QT[0:KS, b * TPB * HEADS * P:(b * TPB + 1) * HEADS * P].rearrange("p (g x) -> p g x", g=HEADS)
                then(nc.vector.tensor_copy(QX[0:KS, b * RX:(b + 1) * RX].rearrange("p (g r) -> p g r", r=REG),
                                           src[:, :, 0:REG]))
            for b in range(BATCH):
                dve.wait_ge(x_ready, b)
                qz = QZ[0:KS, :].rearrange("p (g x) -> p g x", x=RX + REG)
                then(nc.vector.tensor_copy(qz[:, :, 0:REG], QX[0:KS, b * RX:(b + 1) * RX].rearrange(
                    "p (g r) -> p g r", r=REG)))
                nc.vector.memset(QZ[KS:KS + 1, :].rearrange("p (g x) -> p g x", x=RX + REG)[:, :, 0:REG],
                                 NEG).then_inc(qz_ready, 1)
                dve.wait_ge(x_ready, b + 1)
                then(nc.vector.tensor_reduce(mxx[:, b:b + 1], x_ps[:, :], AX.X, ALU.max))
                then(nc.vector.memset(zx[:, b, KS:KS + 1], NEG))
                then(nc.vector.tensor_scalar(zx[:, b, KM:KM + 1], mxx[:, b:b + 1], -1.0, None, ALU.mult))
                nc.vector.scalar_tensor_tensor(zx[:, b, KM + 1:KM + 2], mxx[:, b:b + 1], -1.0,
                                               zx[:, b, KM:KM + 1], ALU.mult, ALU.subtract).then_inc(zx_ready, 1)
            dve.wait_ge(zx_turned, 1)
            then(nc.vector.tensor_copy(QX[KS:KE, :], zx_ps[KS:KE, :]))

        @block.gpsimd
        def _(pool):
            pool.wait_ge(ends_ready, 1)
            nc.gpsimd.partition_all_reduce(endall[:, :], end1[:, :], P, bass.bass_isa.ReduceOp.max).then_inc(ends_all, 1)

        @block.tensor
        def _(pe):
            pe.wait_ge(flags_ready, 1)
            for i in range(4):
                for t in range(TPB):
                    mm = pe.transpose(row_ps[i][:, t * P:(t + 1) * P], rows[:, i // 2, (i % 2) * TPB + t, :],
                                      identb[:, :])
                mm.then_inc(rows_turned, 1)
            pe.wait_ge(spread, 64 * TPB)
            for b in range(BATCH):
                pe.wait_ge(qz_ready, b + 1)
                pe.wait_ge(zx_ready, b)

                def scores(g):
                    for c in range(2):
                        k3 = KT[0:KM, (b * TPB + 4 * c) * HEADS * P:(b * TPB + 4 * c + 4) * HEADS * P].rearrange(
                            "p (t x) -> p t x", t=4)
                        mm = pe.matmul(x_ps[:, c * 512:(c + 1) * 512].rearrange("p (t x) -> p t x", t=4),
                                       QZ[:, at(g * RX, RX)], k3[:, :, at(g * P, P)],
                                       start=isinstance(g, int) and g == 0, stop=isinstance(g, int) and g > 0,
                                       skip_group_check=True)
                    return mm

                scores(0)
                with pe.Fori(1, HEADS - 1) as g:
                    scores(g)
                scores(HEADS - 1).then_inc(x_ready, 1)
            pe.wait_ge(zx_ready, BATCH)
            for b in range(BATCH):
                mm = pe.transpose(zx_ps[:, b * RX:(b + 1) * RX], zx[:, b, :], identb[0:RX, 0:RX])
            mm.then_inc(zx_turned, 1)

        @block.sync
        def _(sp):
            for i in range(4):
                sp.wait_ge(rowT_ready, i + 1)
                b = i % 2
                dst = (KT, QT)[i // 2][KS:KS + 2, b * TPB * HEADS * P:(b + 1) * TPB * HEADS * P].rearrange(
                    "p (t g x) -> p t g x", t=TPB, g=HEADS)
                src = rowT[KS:KS + 2, i // 2, b * TPB * P:(b + 1) * TPB * P].rearrange("p (t x) -> p t x", t=TPB)
                for t in range(TPB):
                    sp.dma_start(dst[:, t], src[:, t].unsqueeze(1).broadcast_to([2, HEADS, P])).then_inc(spread, 16)
            sp.wait_ge(spread, 64 * TPB)


def merge_registers(nc, C, CX):
    with ExitStack() as ctx:
        sb, ps, sem = scope(nc, ctx)
        step = sem("step")
        block = ctx.enter_context(nc.Block())

        @block.vector
        def _(dve):
            for b in range(BATCH):
                rows = C[0:REG, b * TPB * D:b * TPB * D + D]
                nc.vector.tensor_tensor(rows, rows, CX[:, b * D:(b + 1) * D], ALU.add).then_inc(step, 1)
                dve.wait_ge(step, 2 * b + 1)
                nc.vector.tensor_scalar(rows, rows, 0.5, None, ALU.mult).then_inc(step, 1)
                dve.wait_ge(step, 2 * b + 2)


def mixture(nc, h, mean, rstd, const, T, x_scr, y_scr):
    with ExitStack() as ctx:
        sb, ps, sem = scope(nc, ctx)
        HG = GRP // 2
        NG = P // GRP
        CHO = 11
        aT_up = sb("aT_up", [P, E * F1], F32)
        bT_up = sb("bT_up", [P, E * F1], F32)
        aT_dn = sb("aT_dn", [P, E * D1], F32)
        bT_dn = sb("bT_dn", [P, E * D1], F32)
        wr_up = sb("wr_up", [P, 2 * SPM, E], F32)
        wr_dn = sb("wr_dn", [P, F1, E], F32)
        bias_up = sb("bias_up_sb", [F1, F1], F32)
        bias_dn = sb("bias_dn_sb", [D1, D1], F32)
        scales = sb("scales", [F1, 2], F32)
        X = sb("X", [D1, P * D1], F32)
        hid = sb("hid", [P, P * F1], F32)
        yo = sb("yo", [D1, P * D1], F32)
        lo_up = sb("lo_up", [P, NMT * E], F32)
        lo_dnT = sb("lo_dnT", [E, P], F32)
        scores = sb("scores", [P, E], F32)
        vals = sb("vals", [P, 8], F32)
        idx = sb("idx", [P, 8], U32)
        pr = sb("pr", [P, 8], F32)
        dg = sb("dg", [P, 4 * P], F32)
        weight = sb("weight", [F1, P * TOPK], F32)
        offset = sb("offset", [1, P * TOPK], I32)
        xs = [sb(f"xs{i}", [P, HG * D1], F32) for i in range(2)]
        hs = [sb(f"hs{i}", [P, HG * F1], F32) for i in range(2)]
        ts_up = [sb(f"ts_up{i}", [P, HG * TOPK * F1], F32) for i in range(2)]
        ts_dn = [sb(f"ts_dn{i}", [P, HG * TOPK * D1], F32) for i in range(2)]
        pre = [sb(f"pre{i}", [F1, HG * F1], F32) for i in range(2)]
        t_ps = [ps(f"t_ps{i}", [F1, HG * TOPK * F1]) for i in range(2)]
        y_ps = [ps(f"y_ps{i}", [F1, HG * F1]) for i in range(2)]
        r_ps = ps("r_ps", [P, 512])
        b_ps = ps("b_ps", [F1, 4 * P])
        ident = const[:, C_ID:C_ID + P]
        ones = const[:, C_ONES:C_ONES + F1]

        tabs_in, padded = sem("tabs_in"), sem("padded")
        load_tables = [
            (aT_up[0:D1, :], T["up_A"]), (bT_up[0:D1, :], T["up_B"]), (aT_dn[0:F1, :], T["dn_A"]), (bT_dn[0:F1, :], T["dn_B"]),
            (wr_up[:, :, :], T["up_W"].rearrange("(c p) e -> p c e", p=P)),
            (wr_dn[0:F1, :, :], T["dn_W"].rearrange("(o q) e -> o q e", o=F1)),
            (bias_up[:, :], T["up_bias"].rearrange("(o q) -> o q", o=F1)),
            (bias_dn[:, :], T["dn_bias"].rearrange("(o q) -> o q", o=D1)),
            (scales[:, 0:1], T["up_scale"].rearrange("(a b) -> a b", a=1).broadcast_to([F1, 1])),
            (scales[:, 1:2], T["dn_scale"].rearrange("(a b) -> a b", a=1).broadcast_to([F1, 1])),
        ]

        TABS = 16 * len(load_tables)

        with ExitStack() as part1:
            def sb1(name, shape, dt):
                return part1.enter_context(nc.sbuf_tensor(name, shape, dt))

            def ps1(name, shape, dt=F32):
                return part1.enter_context(nc.psum_tensor(name, shape, dt))

            def sem1(name):
                return part1.enter_context(nc.semaphore(name))

            xn = [sb1(f"m_xn{i}", [P, D], F32) for i in range(4)]
            xT = sb1("m_xT", [P, 2, 4 * P], F32)
            xT_ps = [ps1(f"m_xT_ps{i}", [P, D]) for i in range(2)]
            xT_ready = [sem1("xT_ready0"), sem1("xT_ready1")]
            xn_ready, xn_out, turned, logits_ready, logits_out = (
                sem1("xn_ready"), sem1("xn_out"), sem1("turned"), sem1("logits_ready"),
                sem1("logits_out"))
            block = part1.enter_context(nc.Block())

            @block.sync
            def _(sp):
                for dst, src in load_tables:
                    sp.dma_start(dst, src).then_inc(tabs_in, 16)
                with sp.Fori(0, NMT) as m:
                    for i in range(4):
                        sp.wait_ge(xn_ready, m * 4 + (i + 1))
                        sp.dma_start(x_scr[at(m * 4 * P + i * P, P), :], xn[i][:, :]).then_inc(xn_out, 16)
                sp.wait_ge(xn_out, 16 * NT)
                sp.wait_ge(tabs_in, TABS)

            @block.gpsimd
            def _(pool):
                low = ([(x, D1) for x in (aT_up, bT_up, *xs, *ts_up)]
                       + [(x, F1) for x in (aT_dn, bT_dn, wr_dn.rearrange("p q e -> p (q e)"), hid, *hs, *ts_dn)])
                spans = [(x, a, b) for x, rows in low for a, b in ((D1, F1), (F1, P)) if a >= rows]
                for x, a, b in spans:
                    nc.gpsimd.memset(x[a:b, :], 0.0).then_inc(padded, 1)
                pool.wait_ge(padded, len(spans))

            @block.vector
            def _(dve):
                with dve.Fori(0, NMT) as m:
                    for i in range(4):
                        dve.wait_ge(xn_out, (m * 4 + i) * 16)
                        dve.wait_ge(turned, m * 4 + i)
                        nc.vector.tensor_scalar(xn[i][:, :], h[:, at(m * 4 * D + i * D, D)],
                                                mean[:, at(m * 4 + i, 1)], rstd[:, at(m * 4 + i, 1)],
                                                ALU.subtract, ALU.mult).then_inc(xn_ready, 1)
                dve.wait_ge(xn_ready, NT)

            @block.tensor
            def _(pe):
                pe.wait_ge(tabs_in, TABS)
                with pe.Fori(0, NMT) as m:
                    for i in range(4):
                        pe.wait_ge(xn_ready, m * 4 + (i + 1))
                        pe.wait_ge(xT_ready[i % 2], m * 2 + i // 2)
                        for c in range(2):
                            mm = pe.transpose(xT_ps[i % 2][:, c * P:(c + 1) * P], xn[i][:, c * P:(c + 1) * P], ident)
                        mm.then_inc(turned, 1)
                    for i in range(2):
                        pe.wait_ge(xT_ready[i], m * 2 + 2)
                    pe.wait_ge(logits_out, m)
                    for s in range(SPM):
                        for c in range(2):
                            mm = pe.matmul(r_ps[:, 0:E], xT[:, c, s:4 * P:SPM], wr_up[:, 2 * s + c, :],
                                           start=s + c == 0, stop=s + c == SPM)
                    mm.then_inc(logits_ready, 1)

            @block.scalar
            def _(act):
                with act.Fori(0, NMT) as m:
                    for i in range(4):
                        act.wait_ge(turned, m * 4 + (i + 1))
                        act.wait_ge(logits_ready, m)
                        nc.scalar.copy(xT[:, :, i * P:(i + 1) * P],
                                       xT_ps[i % 2][:, :].rearrange("p (c x) -> p c x", c=2)).then_inc(xT_ready[i % 2], 1)
                    act.wait_ge(logits_ready, m + 1)
                    nc.scalar.copy(lo_up[:, part(m, E)], r_ps[:, 0:E]).then_inc(logits_out, 1)
                act.wait_ge(logits_out, NMT)

        step, diag_ready, spread, offset_ready, gap_ready, gap_exp = (
            sem("step"), sem("diag_ready"), sem("spread"), sem("offset_ready"), sem("gap_ready"), sem("gap_exp"))
        x_in = sem("x_in")
        waited, waited_pe = sem("waited"), sem("waited_pe")
        staged = [sem("staged0"), sem("staged1")]
        t_ready = [sem("t_ready0"), sem("t_ready1")]
        ts_ready = [sem("ts_ready0"), sem("ts_ready1")]
        y_ready = [sem("y_ready0"), sem("y_ready1")]
        y_read = [sem("y_read0"), sem("y_read1")]
        gelu_done, dn_scores, dn_copied, dn_logits, choice_read, yo_out = (
            [sem("gelu_done0"), sem("gelu_done1")], sem("dn_scores"), sem("dn_copied"), sem("dn_logits"), sem("choice_read"), sem("yo_out"))
        block = ctx.enter_context(nc.Block())

        def number(m, u, g):
            return m * (2 * NG) + (g + u * NG)

        @block.gpsimd
        def _(pool):
            with pool.Fori(0, NMT) as m:
                for u in range(2):
                    with pool.Fori(0, NG) as g:
                        for i in range(2):
                            n = number(m, u, g)
                            pool.wait_ge(t_ready[i], n)
                            if u == 0:
                                pool.wait_ge(x_in, m * 16 + 16)
                                nc.gpsimd.tensor_copy(xs[i][0:D1, :], X[:, at(g * GRP * D1 + i * HG * D1, HG * D1)]
                                                      ).then_inc(staged[i], 1)
                            else:
                                pool.wait_ge(gelu_done[i], m * NG + g + 1)
                                nc.gpsimd.tensor_copy(hs[i][0:F1, :], hid[0:F1, at(g * GRP * F1 + i * HG * F1, HG * F1)]
                                                      ).then_inc(staged[i], 1)

        @block.tensor
        def _(pe):
            def spread_choice(c):
                pe.wait_ge(diag_ready, c + 1)
                pe.wait_ge(offset_ready, c)
                pe.matmul(b_ps[:, :], ones, dg[:, :], start=True, stop=True).then_inc(spread, 1)

            def experts(m, u, g):
                n = number(m, u, g)
                N1, N2 = (F1, F1) if u == 0 else (D1, D1)
                ta, tb = (aT_up, bT_up) if u == 0 else (aT_dn, bT_dn)
                side = D1 if u == 0 else F1
                stage, ts = (xs, ts_up) if u == 0 else (hs, ts_dn)
                ROWS = D1 if u == 0 else F1
                _, offs = nc.values_load_multi_w_load_instructions(
                    offset[0:1, at(g * GRP * TOPK, GRP * TOPK)], engines=[mybir.EngineType.PE], min_val=0,
                    max_val=(E - 1) * N1, skip_runtime_bounds_check_because="max_index returns 0 to E - 1")
                for i in range(2):
                    pe.wait_ge(staged[i], n + 1)
                    pe.wait_ge(ts_ready[i], n)
                    for q in range(HG):
                        for k in range(TOPK):
                            j = q * TOPK + k
                            mm = pe.matmul(t_ps[i][0:ROWS, j * N1:(j + 1) * N1], stage[i][:, q * side:(q + 1) * side],
                                           ta[:, at(offs[i * HG * TOPK + j], N1)], start=True, stop=True)
                    mm.then_inc(t_ready[i], 1)
                for i in range(2):
                    pe.wait_ge(ts_ready[i], n + 1)
                    pe.wait_ge(y_read[i], n)
                    for q in range(HG):
                        for k in range(TOPK):
                            j = q * TOPK + k
                            mm = pe.matmul(y_ps[i][0:N1, q * N2:(q + 1) * N2], ts[i][:, j * N1:(j + 1) * N1],
                                           tb[:, at(offs[i * HG * TOPK + j], N2)], start=k == 0, stop=k == TOPK - 1)
                    mm.then_inc(y_ready[i], 1)

            with pe.Fori(0, NMT) as m:
                for u in range(2):
                    if u == 1:
                        for i in range(2):
                            pe.wait_ge(gelu_done[i], m * NG + NG)
                        pe.wait_ge(choice_read, m * 4)
                        h3 = hid[:, :].rearrange("p (n q) -> p n q", q=F1)
                        for q in range(F1):
                            mm = pe.matmul(r_ps[0:E, 0:P], wr_dn[:, q, :], h3[:, :, q], start=q == 0, stop=q == F1 - 1)
                        mm.then_inc(dn_scores, 1)
                        pe.wait_ge(dn_copied, m + 1)
                        pe.sem_inc(waited_pe, 1)
                        pe.transpose(r_ps[:, P:P + E], lo_dnT[:, :], const[0:E, C_ID:C_ID + E]).then_inc(dn_logits, 1)
                    spread_choice(m * 2 + u)
                    pe.wait_ge(offset_ready, m * 2 + (u + 1))
                    pe.sem_inc(waited_pe, 1)
                    with pe.Fori(0, NG) as g:
                        experts(m, u, g)

        @block.vector
        def _(dve):
            def choose_two(m, u):
                c = m * 2 + u
                if u == 0:
                    logits = lo_up[:, part(m, E)]
                else:
                    dve.wait_ge(dn_scores, m + 1)
                    nc.vector.tensor_copy(lo_dnT[:, :], r_ps[0:E, 0:P]).then_inc(dn_copied, 1)
                    dve.wait_ge(dn_logits, m + 1)
                    logits = r_ps[:, P:P + E]
                base = [c * CHO]

                def then(ins):
                    base[0] = base[0] + 1
                    ins.then_inc(step, 1)
                    dve.wait_ge(step, base[0])

                nc.vector.tensor_copy(scores[:, :], logits).then_inc(choice_read, 1)
                dve.wait_ge(choice_read, c * 2 + 1)
                dve.sem_inc(waited, 1)
                then(nc.vector.max(out=vals[:, :], in_=scores[:, :]))
                dve.sem_inc(waited, 1)
                nc.vector.max_index(out=idx[:, :], in_max=vals[:, :], in_values=scores[:, :]).then_inc(choice_read, 1)
                dve.wait_ge(choice_read, c * 2 + 2)
                nc.vector.tensor_tensor(pr[:, 0:1], vals[:, 1:2], vals[:, 0:1], ALU.subtract).then_inc(gap_ready, 1)
                then(nc.vector.tensor_copy(pr[:, 4:6], idx[:, 0:2]))
                dve.wait_ge(gap_exp, c + 1)
                then(nc.vector.tensor_scalar(pr[:, 2:3], pr[:, 1:2], 1.0, None, ALU.add))
                then(nc.vector.reciprocal(pr[:, 2:3], pr[:, 2:3]))
                then(nc.vector.tensor_tensor(pr[:, 3:4], pr[:, 1:2], pr[:, 2:3], ALU.mult))
                dve.wait_ge(spread, c)
                for k in range(2):
                    then(nc.vector.tensor_scalar(dg[:, k * P:(k + 1) * P], ident, pr[:, 2 + k:3 + k], None, ALU.mult))
                for k in range(2):
                    then(nc.vector.tensor_scalar(dg[:, (2 + k) * P:(3 + k) * P], ident, pr[:, 4 + k:5 + k],
                                                 None, ALU.mult))
                dve.sem_inc(diag_ready, 1)
                dve.wait_ge(spread, c + 1)
                b3 = b_ps[:, :].rearrange("p (k n) -> p n k", k=4)
                then(nc.vector.tensor_copy(weight[:, :].rearrange("p (n k) -> p n k", k=TOPK), b3[:, :, 0:TOPK]))
                then(nc.vector.tensor_scalar(offset[:, :].rearrange("p (n k) -> p n k", k=TOPK), b3[0:1, :, TOPK:2 * TOPK],
                                             float(F1 if u == 0 else D1), None, ALU.mult))
                dve.sem_inc(offset_ready, 1)

            def weigh(m, u, g, i):
                n = number(m, u, g)
                ROWS, N1, ts = (D1, F1, ts_up) if u == 0 else (F1, D1, ts_dn)
                W = HG * TOPK
                dve.wait_ge(t_ready[i], n + 1)
                dve.wait_ge(y_ready[i], n)
                nc.vector.tensor_tensor(
                    ts[i][0:ROWS, 0:W * N1].rearrange("p (j x) -> p j x", j=W),
                    t_ps[i][0:ROWS, 0:W * N1].rearrange("p (j x) -> p j x", j=W),
                    weight[0:ROWS, at(g * GRP * TOPK + i * W, W)].unsqueeze(2).broadcast_to([ROWS, W, N1]),
                    ALU.mult).then_inc(ts_ready[i], 1)

            def result(m, u, g, i):
                n = number(m, u, g)
                dve.wait_ge(y_ready[i], n + 1)
                if u == 0:
                    dve.wait_ge(gelu_done[i], m * NG + g)
                    nc.vector.scalar_tensor_tensor(
                        pre[i][:, :].rearrange("p (n x) -> p n x", x=F1), y_ps[i][:, :].rearrange("p (n x) -> p n x", x=F1),
                        scales[:, 0:1], bias_up[:, :].unsqueeze(1).broadcast_to([F1, HG, F1]),
                        ALU.mult, ALU.add).then_inc(y_read[i], 1)
                else:
                    nc.vector.scalar_tensor_tensor(
                        yo[:, at(g * GRP * D1 + i * HG * D1, HG * D1)].rearrange("p (n x) -> p n x", x=D1),
                        y_ps[i][0:D1, 0:HG * D1].rearrange("p (n x) -> p n x", x=D1),
                        scales[0:D1, 1:2], bias_dn[:, :].unsqueeze(1).broadcast_to([D1, HG, D1]),
                        ALU.mult, ALU.add).then_inc(y_read[i], 1)

            with dve.Fori(0, NMT) as m:
                for u in range(2):
                    choose_two(m, u)
                    if u == 1:
                        dve.wait_ge(yo_out, m * 16)
                        dve.sem_inc(waited, 1)
                    with dve.Fori(0, NG) as g:
                        for i in range(2):
                            weigh(m, u, g, i)
                        for i in range(2):
                            result(m, u, g, i)

        @block.scalar
        def _(act):
            def gap(c):
                act.wait_ge(gap_ready, c + 1)
                nc.scalar.activation(pr[:, 1:2], pr[:, 0:1], ACT.Exp).then_inc(gap_exp, 1)

            with act.Fori(0, NMT) as m:
                gap(m * 2)
                with act.Fori(0, NG) as g:
                    for i in range(2):
                        n = number(m, 0, g)
                        act.wait_ge(y_read[i], n + 1)
                        act.wait_ge(t_ready[i], n)
                        nc.scalar.activation(hid[0:F1, at(g * GRP * F1 + i * HG * F1, HG * F1)], pre[i][:, :],
                                             ACT.Gelu).then_inc(gelu_done[i], 1)
                gap(m * 2 + 1)

        @block.sync
        def _(sp):
            y3 = y_scr.rearrange("(n s) f -> n (s f)", s=SPM)
            x3 = x_scr.rearrange("(n s) f -> n (s f)", s=SPM)

            def load(m):
                sp.dma_start(X[:, :].rearrange("i (n j) -> i n j", j=D1),
                             x3[at(m * P, P), :].rearrange("n (i j) -> i n j", j=D1)).then_inc(x_in, 16)

            def store(m):
                for i in range(2):
                    sp.wait_ge(y_read[i], m * (2 * NG) + 2 * NG)
                sp.dma_start(y3[at(m * P, P), :].rearrange("n (o q) -> o n q", q=D1),
                             yo[:, :].rearrange("p (n x) -> p n x", x=D1)).then_inc(yo_out, 16)

            load(0)
            with sp.Fori(0, NMT - 1) as m:
                for i in range(2):
                    sp.wait_ge(staged[i], m * (2 * NG) + NG)
                load(m + 1)
                store(m)
            store(NMT - 1)
            sp.wait_ge(yo_out, 16 * NMT)


def add_mixture(nc, h, y_scr, out_dram=None):
    with ExitStack() as ctx:
        sb, ps, sem = scope(nc, ctx)
        y = sb("am_y", [P, NT * D], F32)
        y_in, added, stored = [sem(f"y_in{c}") for c in range(4)], sem("added"), sem("stored")
        block = ctx.enter_context(nc.Block())

        @block.sync
        def _(sp):
            for c in range(4):
                sp.dma_start(y[:, part(c, 4 * D)].rearrange("p (t d) -> p t d", d=D),
                             y_scr[part(c, 4 * P), :].rearrange("(t p) d -> p t d", p=P)).then_inc(y_in[c], 16)
            for c in range(4):
                sp.wait_ge(y_in[c], 16)
            if out_dram is not None:
                sp.wait_ge(added, 4)
                sp.dma_start(out_dram.rearrange("b (t p) d -> p (b t) d", p=P),
                             h[:, :].rearrange("p (t d) -> p t d", d=D)).then_inc(stored, 16)
                sp.wait_ge(stored, 16)

        @block.vector
        def _(dve):
            for c in range(4):
                dve.wait_ge(y_in[c], 16)
                hs = h[:, part(c, 4 * D)]
                nc.vector.tensor_tensor(hs, hs, y[:, part(c, 4 * D)], ALU.add).then_inc(added, 1)
            dve.wait_ge(added, 4)


def tower(nc, T, out, upto=99):
    with ExitStack() as ctx:
        def sb(name, shape, dt):
            return ctx.enter_context(nc.sbuf_tensor(name, shape, dt))

        h = sb("h", [P, NT * D], F32)
        const = sb("const_sb", [P, C_W], F32)
        identb = sb("identb", [P, P], BF16)
        ids = sb("ids_sb", [P, NT], I32)
        mean = sb("mean", [P, NT], F32)
        rstd = sb("rstd", [P, NT], F32)
        rows_in = ctx.enter_context(nc.semaphore("rows_in"))
        x_scr = nc.dram_tensor("x_scr", (TOK, D), F32, kind="Internal").ap()
        y_scr = nc.dram_tensor("y_scr", (TOK, D), F32, kind="Internal").ap()

        def attention(n, grouped=False, out_dram=None):
            with ExitStack() as layer:
                def lsb(name, shape, dt):
                    return layer.enter_context(nc.sbuf_tensor(f"L{n}_{name}", shape, dt))
                QT = lsb("QT", [KS + 4, NT * HEADS * P], BF16)
                KT = lsb("KT", [KS + 4, NT * HEADS * P], BF16)
                V = lsb("V", [P, NT * D], F32)
                if n == 0:
                    embed(nc, h, const, identb, KT, ids, rows_in, T["ids"], T["tok_W"], T["const"])
                else:
                    set_ones(nc, KT)
                gauge = extra = None
                if grouped:
                    CX = lsb("CX", [REG, BATCH * D], F32)
                    QX = lsb("QX", [KS + 4, BATCH * HEADS * REG], BF16)
                    pen = lsb("pen", [P, NT * 2], BF16)
                    with ExitStack() as g:
                        gq = g.enter_context(nc.sbuf_tensor("gq", [P, D], F32))
                        gdot = g.enter_context(nc.sbuf_tensor("gdot", [P, NT * HEADS], F32))
                        gnorm = g.enter_context(nc.sbuf_tensor("gnorm", [P, NT * HEADS], F32))
                        gauge_vector(nc, gq, T["g_info"])
                        statistics(nc, h, mean, rstd, f"L{n}s")
                        project(nc, h, mean, rstd, const, identb, T[f"L{n}_Wqk"], T[f"L{n}_Wv"], QT, KT, V, False,
                                f"L{n}p", (gq, gdot, gnorm))
                        group_tokens(nc, const, identb, gdot, gnorm, QT, KT, QX, pen)
                    extra = (QX, CX, pen)
                else:
                    statistics(nc, h, mean, rstd, f"L{n}s")
                    project(nc, h, mean, rstd, const, identb, T[f"L{n}_Wqk"], T[f"L{n}_Wv"], QT, KT, V, True, f"L{n}p")
                C = lsb("C", [P, NT * D], F32)
                attend(nc, const, identb, QT, KT, V, C, not grouped, f"L{n}a", extra)
                if grouped:
                    merge_registers(nc, C, CX)
                project_out(nc, h, C, const, T[f"L{n}_Wo"], f"L{n}o", T["L2_bias"] if grouped else None, out_dram)

        attention(0, out_dram=out if upto == 1 else None)
        if upto == 1:
            return
        statistics(nc, h, mean, rstd, "Ms")
        mixture(nc, h, mean, rstd, const, T, x_scr, y_scr)
        add_mixture(nc, h, y_scr, out if upto == 2 else None)
        if upto == 2:
            return
        recycle(nc)
        attention(1, out_dram=out if upto == 3 else None)
        if upto == 3:
            return
        recycle(nc)
        attention(2, True, out)


INPUTS = {
    "ids": ((P, NT), I32), "tok_W": ((50257, D), F32), "const": ((P, C_W), F32),
    **{f"L{n}_{w}": ((D, QK if w == "Wqk" else D), F32) for n in range(3) for w in ("Wqk", "Wv", "Wo")},
    "L2_bias": ((D,), F32), "g_info": ((12, 2, D), F32),
    "up_A": ((D1, E * F1), F32), "up_B": ((D1, E * F1), F32), "dn_A": ((F1, E * D1), F32), "dn_B": ((F1, E * D1), F32),
    "up_W": ((D1 * D1, E), F32), "dn_W": ((F1 * F1, E), F32), "up_bias": ((F1 * F1,), F32), "dn_bias": ((D1 * D1,), F32),
    "up_scale": ((1,), F32), "dn_scale": ((1,), F32),
}


def constants():
    import numpy as np
    c = np.zeros((P, C_W), np.float32)
    i = np.arange(P)
    c[:, C_ID:C_ID + P] = np.eye(P)
    c[:, C_MASK:C_MASK + P] = np.where(i[None, :] > i[:, None], NEG, 0)
    c[:, C_MASKT:C_MASKT + P] = np.where(i[None, :] < i[:, None], NEG, 0)
    inv = np.float32(1.0) / np.float32(10000.0) ** (np.arange(0, HD, 2, dtype=np.float32) / np.float32(HD))
    ang = np.arange(SEQ, dtype=np.float32)[:, None] * inv.astype(np.float32)[None, :]
    cos = np.repeat(np.cos(ang), 2, axis=1)
    sin = np.stack([-np.sin(ang), np.sin(ang)], axis=-1).reshape(SEQ, HD)
    for base, table in ((C_COS, cos), (C_SIN, sin)):
        c[:, base:base + TPB * HD] = table.reshape(TPB, P, HD).transpose(1, 0, 2).reshape(P, TPB * HD)
    reg = np.zeros((P, NT), bool)
    reg[0:REG, ::TPB] = True
    c[:, C_REG:C_REG + NT] = np.where(reg, NEG, 0)
    c[:, C_TOKM:C_TOKM + NT] = ~reg
    c[:, C_ONES:C_ONES + P] = 1.0
    return c


def kernel(**inputs):
    import numpy as _np
    import concourse.bacc as _bacc
    from concourse.bass_utils import run_bass_kernel_spmd as _run

    def flat(a):
        return _np.ascontiguousarray(_np.asarray(a))

    g = inputs
    W = {
        "ids": flat(_np.asarray(g["x"]).reshape(NT, P).T),
        "tok_W": flat(_np.asarray(g["L0_tok_W"]).T),
        "const": constants(),
    }
    for n in (0, 1):
        W[f"L{n}_Wqk"] = flat(_np.concatenate([_np.asarray(g[f"L{n}_attn_Wq"]).T, _np.asarray(g[f"L{n}_attn_Wk"]).T], axis=1))
        W[f"L{n}_Wv"] = flat(_np.asarray(g[f"L{n}_attn_Wv"]).T)
        W[f"L{n}_Wo"] = flat(_np.asarray(g[f"L{n}_attn_Wo"]).T)
    W["L2_Wqk"] = flat(_np.asarray(g["L1_ffn_W_qkv"])[:, :QK])
    W["L2_Wv"] = flat(_np.asarray(g["L1_ffn_W_qkv"])[:, QK:])
    W["L2_Wo"] = flat(g["L1_ffn_W_proj"])
    W["L2_bias"] = flat(g["L1_ffn_b_proj"])
    W["g_info"] = flat(g["L1_ffn_g_info"])
    for key, name in (("up", "L0_ffn_{}_up"), ("dn", "L0_ffn_{}_down")):
        for w in "AB":
            a = _np.asarray(g[name.format(w)])
            W[f"{key}_{w}"] = flat(a.transpose(2, 0, 1).reshape(a.shape[2], -1))
        W[f"{key}_W"] = flat(_np.asarray(g[name.format("W")]).T)
        W[f"{key}_bias"] = flat(g[name.format("bias")])
        W[f"{key}_scale"] = flat(g[name.format("scale")])
    nc = _bacc.Bacc("TRN2", target_bir_lowering=False, num_devices=1)
    T = {n: nc.dram_tensor(n, shape, dt, kind="ExternalInput").ap() for n, (shape, dt) in INPUTS.items()}
    out = nc.dram_tensor("out", (BATCH, SEQ, D), F32, kind="ExternalOutput").ap()
    tower(nc, T, out)
    r = _run(nc, [W], core_ids=[0])
    return r.results[0]["out"]
```

```python
from contextlib import ExitStack

import concourse.bass as bass
from concourse import mybir

F32 = mybir.dt.float32
BF16 = mybir.dt.bfloat16
I32 = mybir.dt.int32
U32 = mybir.dt.uint32
ALU = mybir.AluOpType
ACT = mybir.ActivationFunctionType
AX = mybir.AxisListType

P = 128
BATCH, SEQ, D = 2, 1024, 256
HEADS, HD = 16, 16
TOK = BATCH * SEQ
NT = TOK // P
TPB = SEQ // P
QK = 2 * D
COMPS = 6
KS = COMPS * HD
REG = 5
NEG = -1e30
SCALE = HD ** -0.5
EPS = 1e-5
E = 64
TOPK = 2
D1, F1 = 32, 64
SPM = D1 * D1 // D
NM = TOK // SPM
NMT = NM // P
GRP = 8
LAST = HD + 16

C_ID, C_MASK, C_MASKT, C_COS, C_SIN, C_REG, C_TOKM = 0, 128, 256, 384, 512, 640, 656
C_ONES, C_W = 688, 816


def scope(nc, ctx):
    def sb(name, shape, dt):
        return ctx.enter_context(nc.sbuf_tensor(name, shape, dt))

    def ps(name, shape, dt=F32):
        return ctx.enter_context(nc.psum_tensor(name, shape, dt))

    def sem(name):
        return ctx.enter_context(nc.semaphore(name))

    return sb, ps, sem


def part(i, n):
    return slice(i * n, (i + 1) * n) if isinstance(i, int) else bass.ds(i * n, n)


def at(i, n):
    return slice(i, i + n) if isinstance(i, int) else bass.ds(i, n)


def recycle(nc):
    ids = sorted(nc.released_uncleared_semaphores)
    start = 0
    for i in range(1, len(ids) + 1):
        if i == len(ids) or ids[i] != ids[i - 1] + 1:
            nc.sync.sem_clear(range(ids[start], ids[i - 1] + 1))
            start = i
    nc.all_engine_barrier()


def embed(nc, h, const, identb, ids, rows_in, ids_dram, table, const_dram):
    with ExitStack() as ctx:
        sb, ps, sem = scope(nc, ctx)
        ids_in, const_in, made = sem("ids_in"), sem("const_in"), sem("made")
        block = ctx.enter_context(nc.Block())

        @block.sync
        def _(sp):
            sp.dma_start(ids[:, :], ids_dram).then_inc(ids_in, 16)
            sp.dma_start(const[:, :], const_dram).then_inc(const_in, 16)
            sp.wait_ge(const_in, 16)

        @block.vector
        def _(dve):
            dve.wait_ge(const_in, 16)
            nc.vector.tensor_copy(identb[:, :], const[:, C_ID:C_ID + P]).then_inc(made, 1)
            dve.wait_ge(made, 1)

        @block.gpsimd
        def _(pool):
            pool.wait_ge(ids_in, 16)
            for t in range(NT):
                nc.gpsimd.indirect_dma_start(
                    out=h[:, t * D:(t + 1) * D], out_offset=None, in_=table,
                    in_offset=bass.IndirectOffsetOnAxis(ap=ids[:, t:t + 1], axis=0)).then_inc(rows_in, 16)
            pool.wait_ge(rows_in, 16 * NT)


def statistics(nc, h, mean, rstd, name):
    with ExitStack() as ctx:
        sb, ps, sem = scope(nc, ctx)
        bn = sb(f"{name}_bn", [P, NT * 6], F32)
        mv = sb(f"{name}_mv", [P, NT * 2], F32)
        ve = sb(f"{name}_ve", [P, NT], F32)
        root = sb(f"{name}_root", [P, NT], F32)
        stats_done, var_done, root_done, newton = sem("stats_done"), sem("var_done"), sem("root_done"), sem("newton")
        mv3 = mv[:, :].rearrange("p (t c) -> p t c", c=2)
        block = ctx.enter_context(nc.Block())

        @block.vector
        def _(dve):
            with dve.Fori(0, NT) as t:
                nc.vector.bn_stats(bn[:, part(t, 6)], h[:, part(t, D)]).then_inc(stats_done, 1)
            dve.wait_ge(stats_done, NT)
            for t in range(NT):
                nc.vector.bn_aggr(mv[:, part(t, 2)], bn[:, part(t, 6)]).then_inc(stats_done, 1)
            dve.wait_ge(stats_done, 2 * NT)
            nc.vector.tensor_copy(mean[:, :], mv3[:, :, 0]).then_inc(newton, 1)
            nc.vector.tensor_scalar(ve[:, :], mv3[:, :, 1], EPS, None, ALU.add).then_inc(var_done, 1)
            dve.wait_ge(root_done, 1)
            nc.vector.reciprocal(rstd[:, :], root[:, :]).then_inc(newton, 1)
            dve.wait_ge(newton, 2)
            nc.vector.tensor_tensor(ve[:, :], ve[:, :], rstd[:, :], ALU.mult).then_inc(newton, 1)
            dve.wait_ge(newton, 3)
            nc.vector.tensor_tensor(ve[:, :], ve[:, :], root[:, :], ALU.add).then_inc(newton, 1)
            dve.wait_ge(newton, 4)
            nc.vector.tensor_scalar(ve[:, :], ve[:, :], 0.5, None, ALU.mult).then_inc(newton, 1)
            dve.wait_ge(newton, 5)
            nc.vector.reciprocal(rstd[:, :], ve[:, :]).then_inc(newton, 1)
            dve.wait_ge(newton, 6)

        @block.scalar
        def _(act):
            act.wait_ge(var_done, 1)
            nc.scalar.activation(root[:, :], ve[:, :], ACT.Sqrt).then_inc(root_done, 1)


def project(nc, h, mean, rstd, const, identb, w_qk_dram, w_v_dram, QT, KT, V, rope, name, gauge=None):
    with ExitStack() as ctx:
        sb, ps, sem = scope(nc, ctx)
        wqk = sb(f"{name}_wqk", [P, 2, QK], F32)
        wv = sb(f"{name}_wv", [P, 2, D], F32)
        xn = [sb(f"{name}_xn{i}", [P, D], F32) for i in range(1)]
        xT = sb(f"{name}_xT", [P, D], F32)
        turned = sb(f"{name}_turned", [P, QK], F32)
        cross = sb(f"{name}_cross", [P, QK], F32)
        rest = sb(f"{name}_rest", [P, QK], F32)
        hi = sb(f"{name}_hi", [P, QK], BF16)
        mid = sb(f"{name}_mid", [P, QK], BF16)
        stack = sb(f"{name}_stack", [P, 2, HEADS, KS], BF16)
        ones = sb(f"{name}_ones", [4, HEADS * P], BF16)
        xT_ps = ps(f"{name}_xT_ps", [P, D])
        qk_ps = ps(f"{name}_qk_ps", [P, QK])
        v_ps = ps(f"{name}_v_ps", [P, D])
        st_ps = [ps(f"{name}_st_ps{j}", [P, 8 * P], BF16) for j in range(4)]
        w_in, xn_ready, xT_turned, xT_ready = sem("w_in"), sem("xn_ready"), sem("xT_turned"), sem("xT_ready")
        qkv_ready, v_used = sem("qkv_ready"), sem("v_used")
        turn_part, rot_ready, hi_ready, rest_ready, mid_ready = (
            sem("turn_part"), sem("rot_ready"), sem("hi_ready"), sem("rest_ready"), sem("mid_ready"))
        low_ready, stack_part, stack_turned, bank_used = (
            sem("low_ready"), sem("stack_part"), sem("stack_turned"), sem("bank_used"))
        bank_used_act = sem("bank_used_act")
        gauged, ones_made, ones_spread = sem("gauged"), sem("ones_made"), sem("ones_spread")
        ident = const[:, C_ID:C_ID + P]
        t3 = turned[:, :].rearrange("p (g i c) -> p g i c", g=2 * HEADS, c=2)
        if gauge is not None:
            gq, gdot, gnorm = gauge
            gtmp = sb(f"{name}_gtmp", [P, D], F32)
        block = ctx.enter_context(nc.Block())

        @block.sync
        def _(sp):
            sp.dma_start(wqk[:, :, :], w_qk_dram.rearrange("(c p) n -> p c n", p=P)).then_inc(w_in, 16)
            sp.dma_start(wv[:, :, :], w_v_dram.rearrange("(c p) n -> p c n", p=P)).then_inc(w_in, 16)
            sp.wait_ge(ones_made, 1)
            sp.dma_start(KT[KS:KS + 4, :].rearrange("p (t x) -> p t x", t=NT),
                         ones[:, :].unsqueeze(1).broadcast_to([4, NT, HEADS * P])).then_inc(ones_spread, 16)
            sp.wait_ge(w_in, 32)
            sp.wait_ge(ones_spread, 16)

        @block.tensor
        def _(pe):
            def turn_x(t):
                pe.wait_ge(xn_ready, t + 1)
                for c in range(2):
                    mm = pe.transpose(xT_ps[:, c * P:(c + 1) * P], xn[0][:, c * P:(c + 1) * P], ident)
                mm.then_inc(xT_turned, 1)

            def products(t):
                pe.wait_ge(xT_ready, t + 1)
                pe.wait_ge(rot_ready, t)
                pe.wait_ge(v_used, t)
                for c in range(2):
                    pe.matmul(qk_ps[:, :], xT[:, c * P:(c + 1) * P], wqk[:, c, :], start=c == 0, stop=c == 1)
                for c in range(2):
                    mm = pe.matmul(v_ps[:, :], xT[:, c * P:(c + 1) * P], wv[:, c, :], start=c == 0, stop=c == 1)
                mm.then_inc(qkv_ready, 1)

            def turn_stack(t):
                pe.wait_ge(stack_part, 6 * t + 6)
                pe.wait_ge(low_ready, 2 * t + 2)
                pe.wait_ge(bank_used, 2 * t)
                pe.wait_ge(bank_used_act, 2 * t)
                for j in range(4):
                    for g in range(8):
                        mm = pe.transpose(st_ps[j][0:KS, g * P:(g + 1) * P],
                                          stack[:, j // 2, (j % 2) * 8 + g, :], identb[:, :])
                    mm.then_inc(stack_turned, 1)

            pe.wait_ge(w_in, 32)
            turn_x(0)
            products(0)
            turn_x(1)
            products(1)
            turn_x(2)
            turn_stack(0)
            with pe.Fori(2, NT - 1) as t:
                products(t)
                turn_x(t + 1)
                turn_stack(t - 1)
            products(NT - 1)
            turn_stack(NT - 2)
            turn_stack(NT - 1)

        @block.vector
        def _(dve):
            def norm(t):
                dve.wait_ge(xT_turned, t)
                nc.vector.tensor_scalar(xn[0][:, :], h[:, part(t, D)], mean[:, part(t, 1)],
                                        rstd[:, part(t, 1)], ALU.subtract, ALU.mult).then_inc(xn_ready, 1)

            def rotate(t, t_in_batch):
                dve.wait_ge(qkv_ready, t + 1)
                if rope:
                    cos = const[:, at(t_in_batch * HD + C_COS, HD)].unsqueeze(1).broadcast_to([P, 2 * HEADS, HD])
                    dve.wait_ge(rest_ready, t)
                    nc.vector.tensor_tensor(turned[:, :].rearrange("p (g d) -> p g d", d=HD),
                                            qk_ps[:, :].rearrange("p (g d) -> p g d", d=HD),
                                            cos, ALU.mult).then_inc(turn_part, 1)
                    q4 = qk_ps[:, :].rearrange("p (g i c) -> p g i c", i=HD // 2, c=2)
                    c4 = cross[:, :].rearrange("p (g i c) -> p g i c", i=HD // 2, c=2)
                    for c in range(2):
                        sin = const[:, at(t_in_batch * HD + C_SIN, HD)].rearrange(
                            "p (i c) -> p i c", c=2)[:, :, c].unsqueeze(1).broadcast_to([P, 2 * HEADS, HD // 2])
                        nc.vector.tensor_tensor(c4[:, :, :, c], q4[:, :, :, 1 - c], sin, ALU.mult).then_inc(turn_part, 1)
                    dve.wait_ge(turn_part, 3 * t + 3)
                    nc.vector.tensor_tensor(turned[:, :], turned[:, :], cross[:, :], ALU.add).then_inc(rot_ready, 1)
                else:
                    dve.wait_ge(rest_ready, t)
                    nc.vector.tensor_copy(turned[:, :], qk_ps[:, :]).then_inc(rot_ready, 1)
                    dve.wait_ge(rot_ready, t + 1)
                    nc.vector.tensor_tensor(gtmp[:, :], turned[:, 0:D], turned[:, 0:D], ALU.mult).then_inc(gauged, 1)
                    dve.wait_ge(gauged, 4 * t + 1)
                    nc.vector.tensor_reduce(gnorm[:, part(t, HEADS)],
                                            gtmp[:, :].rearrange("p (g d) -> p g d", d=HD), AX.X, ALU.add).then_inc(gauged, 1)
                    dve.wait_ge(gauged, 4 * t + 2)
                    nc.vector.tensor_tensor(gtmp[:, :], turned[:, 0:D], gq[:, :], ALU.mult).then_inc(gauged, 1)
                    dve.wait_ge(gauged, 4 * t + 3)
                    nc.vector.tensor_reduce(gdot[:, part(t, HEADS)],
                                            gtmp[:, :].rearrange("p (g d) -> p g d", d=HD), AX.X, ALU.add).then_inc(gauged, 1)
                    dve.wait_ge(gauged, 4 * t + 4)

            def assemble(t):
                s5 = stack[:, :, :, :].rearrange("p a g (c d) -> p a g c d", d=HD)
                h4 = hi[:, :].rearrange("p (a g d) -> p a g d", a=2, d=HD)
                m4 = mid[:, :].rearrange("p (a g d) -> p a g d", a=2, d=HD)
                dve.wait_ge(hi_ready, t + 1)
                dve.wait_ge(stack_turned, 4 * t)
                for a, lo in ((0, 0), (1, 2)):
                    nc.vector.tensor_copy(s5[:, a, :, lo:lo + 3, :],
                                          h4[:, a].unsqueeze(2).broadcast_to([P, HEADS, 3, HD])).then_inc(stack_part, 1)
                dve.wait_ge(mid_ready, t + 1)
                for a, cs in ((0, (3, 5)), (1, (0, 5))):
                    for c in cs:
                        nc.vector.tensor_copy(s5[:, a, :, c, :], m4[:, a]).then_inc(stack_part, 1)

            def copy_out(t):
                for j in range(2):
                    dve.wait_ge(stack_turned, 4 * t + j + 1)
                    nc.vector.tensor_copy(QT[0:KS, at(t * HEADS * P + j * 8 * P, 8 * P)],
                                          st_ps[j][0:KS, :]).then_inc(bank_used, 1)

            def tile(b, tb, first=False, last=False):
                t = tb + b * TPB
                if not last:
                    norm(t + 1)
                rotate(t, tb)
                if not first:
                    copy_out(t - 1)
                assemble(t)

            nc.vector.memset(ones[:, :], 1.0).then_inc(ones_made, 1)
            norm(0)
            tile(0, 0, first=True)
            tile(0, 1)
            with dve.Fori(2, TPB) as tb:
                tile(0, tb)
            with dve.Fori(0, TPB - 1) as tb:
                tile(1, tb)
            tile(1, TPB - 1, last=True)
            copy_out(NT - 1)
            dve.wait_ge(bank_used, 2 * NT)

        @block.scalar
        def _(act):
            def copy_x(t):
                act.wait_ge(xT_turned, t + 1)
                act.wait_ge(qkv_ready, t)
                nc.scalar.copy(xT[:, :], xT_ps[:, :]).then_inc(xT_ready, 1)

            def copy_v(t):
                act.wait_ge(qkv_ready, t + 1)
                nc.scalar.copy(V[:, part(t, D)], v_ps[:, :]).then_inc(v_used, 1)

            def split(t):
                act.wait_ge(rot_ready, t + 1)
                act.wait_ge(stack_part, 6 * t)
                nc.scalar.copy(hi[:, :], turned[:, :]).then_inc(hi_ready, 1)
                act.wait_ge(rest_ready, t + 1)
                act.wait_ge(low_ready, 2 * t)
                nc.scalar.copy(mid[:, :], rest[:, :]).then_inc(mid_ready, 1)

            def copy_out(t):
                for j in range(2):
                    act.wait_ge(stack_turned, 4 * t + j + 3)
                    nc.scalar.copy(KT[0:KS, at(t * HEADS * P + j * 8 * P, 8 * P)],
                                   st_ps[2 + j][0:KS, :]).then_inc(bank_used_act, 1)

            def tile(t, first=False, last=False):
                copy_v(t)
                if not last:
                    copy_x(t + 1)
                split(t)
                if not first:
                    copy_out(t - 1)

            copy_x(0)
            tile(0, first=True)
            tile(1)
            with act.Fori(2, NT - 1) as t:
                tile(t)
            tile(NT - 1, last=True)
            copy_out(NT - 1)
            act.wait_ge(bank_used_act, 2 * NT)

        @block.gpsimd
        def _(pool):
            def tile(t):
                pool.wait_ge(hi_ready, t + 1)
                pool.wait_ge(low_ready, 2 * t)
                nc.gpsimd.tensor_tensor(rest[:, :], turned[:, :], hi[:, :], ALU.subtract).then_inc(rest_ready, 1)
                pool.wait_ge(mid_ready, t + 1)
                pool.wait_ge(stack_turned, 4 * t)
                s5 = stack[:, :, :, :].rearrange("p a g (c d) -> p a g c d", d=HD)
                r4 = rest[:, :].rearrange("p (a g d) -> p a g d", a=2, d=HD)
                m4 = mid[:, :].rearrange("p (a g d) -> p a g d", a=2, d=HD)
                for a, c in ((0, 4), (1, 1)):
                    nc.gpsimd.tensor_tensor(s5[:, a, :, c, :], r4[:, a], m4[:, a], ALU.subtract).then_inc(low_ready, 1)

            tile(0)
            with pool.Fori(1, NT) as t:
                tile(t)


def attend(nc, const, identb, QT, KT, V, ctx_out, causal, name, extra=None):
    with ExitStack() as ctx:
        sb, ps, sem = scope(nc, ctx)
        CHUNKS = [(qt, c) for qt in range(TPB) for c in range((qt if causal else TPB - 1) // 4 + 1)]
        NCH = len(CHUNKS)
        HALF = NCH // 2
        KM = KS + (0 if causal else 2)
        KE = KM + 2
        G = TPB // 2
        AHEAD = 6
        BEFORE = [(0, 1), (1, 1), (1, 1), (1, 0), (0, 2), (1, 1), (1, 1), (0, 0)] if causal else \
            [(0, 1), (1, 1), (1, 1), (1, 1), (1, 1), (1, 1), (1, 1), (1, 2)]
        TURN = 4 if causal else 6
        assert sum(x + y for x, y in BEFORE) == NCH
        maskb = sb(f"{name}_maskb", [P, 2 * P], BF16)
        vst = sb(f"{name}_vst", [P, TPB, 32], F32)
        probs = [sb(f"{name}_probs{i}", [P, SEQ], F32) for i in range(2)]
        mxp = sb(f"{name}_mxp", [P, 2, TPB], F32)
        mx = sb(f"{name}_mx", [P, TPB], F32)
        negm = sb(f"{name}_negm", [P, TPB, KE], BF16)
        oT = sb(f"{name}_oT", [P, 2 * P], F32)
        rec = sb(f"{name}_rec", [P, TPB], F32)
        small = [ps(f"{name}_small{i}", [P, 512]) for i in range(2)]
        wide = [ps(f"{name}_wide{i}", [P, SEQ]) for i in range(2)]
        out_ps = ps(f"{name}_out", [P, 512])
        turn_ps = ps(f"{name}_turn", [P, 512])
        consts_set = sem("consts_set")
        small_filled = [sem("small_filled0"), sem("small_filled1")]
        small_used = [sem("small_used0"), sem("small_used1")]
        scores_ready = [sem("scores_ready0"), sem("scores_ready1")]
        probs_ready = [sem("probs_ready0"), sem("probs_ready1")]
        probs_used = [sem("probs_used0"), sem("probs_used1")]
        mx_ready, hi_set, negm_ready, max_turned, rows_ready = (
            sem("mx_ready"), sem("hi_set"), sem("negm_ready"), sem("max_turned"), sem("rows_ready"))
        v_staged, oT_ready, out_turned, rec_ready, divided = (
            sem("v_staged"), sem("oT_ready"), sem("out_turned"), sem("rec_ready"), sem("divided"))
        ones_set, pen_set = sem("ones_set"), sem("pen_set")
        if extra is not None:
            QX, ctx_x, pen = extra
            probs_x = sb(f"{name}_probs_x", [P, TPB * REG], F32)
            oT_x = sb(f"{name}_oT_x", [32, REG], F32)
            rec_x = sb(f"{name}_rec_x", [REG, 1], F32)
            xscores_ready, xprobs_ready, xout_ready, oT_part, xdone = (
                sem("xscores_ready"), sem("xprobs_ready"), sem("xout_ready"), sem("oT_part"), sem("xdone"))
            XO = 2 * P
        ident = const[:, C_ID:C_ID + P]
        block = ctx.enter_context(nc.Block())

        def tile_of(M, rows, b, r, t):
            return M[rows, at(r * P + (b * TPB + t) * HEADS * P, P)]

        def tiles_of(M, rows, b, r, t0, n):
            m3 = M[rows, (b * TPB + t0) * HEADS * P:(b * TPB + t0 + n) * HEADS * P].rearrange(
                "p (t x) -> p t x", t=n)
            return m3[:, :, at(r * P, P)]

        def num(b, r):
            return r + b * HEADS

        def uses(n, kb):
            return n * (TPB // 2) + kb // 2

        def per_head(eng, body):
            def run(b):
                body(b, 0, True, 2)
                body(b, 1, False, 2)
                with eng.Fori(1, HEADS // 2 - 1) as pair:
                    for i in range(2):
                        body(b, pair * 2 + i, False, 2)
                body(b, HEADS - 2, False, 1)
                body(b, HEADS - 1, False, 0)
            return run

        @block.tensor
        def _(pe):
            def max_scores(b, r, j):
                qt, c = CHUNKS[j]
                bank = j % 2
                tiles = min(4, qt + 1 - 4 * c) if causal else 4
                diag = causal and qt // 4 == c
                pe.wait_ge(small_used[bank], num(b, r) * HALF + j // 2)
                out = small[bank][:, 0:tiles * P].rearrange("p (t x) -> p t x", t=tiles)
                mm = pe.matmul(out, tile_of(QT, slice(0, KM), b, r, qt),
                               tiles_of(KT, slice(0, KM), b, r, 4 * c, tiles), start=True, stop=not diag)
                if diag:
                    mm = pe.matmul(small[bank][:, (tiles - 1) * P:tiles * P], identb[:, :], maskb[:, 0:P],
                                   start=False, stop=True)
                mm.then_inc(small_filled[bank], 1)

            def turn_max(b, r, sums_before):
                pe.wait_ge(negm_ready, num(b, r) + 1)
                pe.wait_ge(divided, sums_before)
                rows = turn_ps[:, :].bitcast(BF16)
                for t in range(TPB):
                    mm = pe.transpose(rows[0:KE, t * P:(t + 1) * P], negm[:, t, :], identb[:, :])
                mm.then_inc(max_turned, 1)

            def exp_scores(b, r, kb):
                w, n = kb % 2, num(b, r)
                first_q = kb if causal else 0
                if kb == 0:
                    pe.wait_ge(rows_ready, n + 1)
                pe.wait_ge(probs_ready[w], uses(n, kb))
                for q0 in range(first_q, TPB, 4):
                    tiles = min(4, TPB - q0)
                    col = (q0 - first_q) * P
                    diag = causal and q0 == kb
                    mm = pe.matmul(wide[w][:, col:col + tiles * P].rearrange("p (t x) -> p t x", t=tiles),
                                   tile_of(KT, slice(0, KE), b, r, kb),
                                   tiles_of(QT, slice(0, KE), b, r, q0, tiles), start=True, stop=not diag)
                    if diag:
                        mm = pe.matmul(wide[w][:, 0:P], identb[:, :], maskb[:, P:2 * P], start=False, stop=True)
                mm.then_inc(scores_ready[w], 1)

            def values(b, r, kb):
                w, n = kb % 2, num(b, r)
                if kb == 0:
                    pe.wait_ge(v_staged, n + 1)
                    pe.wait_ge(oT_ready, n)
                    if extra is not None:
                        extra_values(b, r)
                pe.wait_ge(probs_ready[w], uses(n, kb) + 1)
                first_q = kb if causal else 0
                for g in range(first_q // 2, G):
                    q0, q1 = max(2 * g, first_q), 2 * g + 2
                    mm = pe.matmul(out_ps[32 * g:32 * g + 32, (q0 % 2) * P:2 * P], vst[:, kb, :],
                                   probs[w][:, (q0 - first_q) * P:(q1 - first_q) * P], start=kb == 0,
                                   stop=kb >= 2 * g if causal else kb == TPB - 1, skip_group_check=causal)
                mm.then_inc(probs_used[w], 1)

            def extra_scores(b, r):
                for kb in range(TPB):
                    mm = pe.matmul(turn_ps[:, kb * REG:(kb + 1) * REG], tile_of(KT, slice(0, KE), b, r, kb),
                                   QX[0:KE, part(num(b, r), REG)], start=True, stop=True)
                mm.then_inc(xscores_ready, 1)

            def extra_values(b, r):
                pe.wait_ge(xprobs_ready, num(b, r) + 1)
                for kb in range(TPB):
                    mm = pe.matmul(out_ps[0:32, XO:XO + REG], vst[:, kb, :],
                                   probs_x[:, kb * REG:(kb + 1) * REG], start=kb == 0, stop=kb == TPB - 1)
                mm.then_inc(xout_ready, 1)

            def turn_out(n):
                pe.wait_ge(oT_ready, n + 1)
                for c in range(2):
                    mm = pe.transpose(turn_ps[:, c * P:(c + 1) * P], oT[:, c * P:(c + 1) * P], ident)
                if extra is not None:
                    mm = pe.transpose(turn_ps[0:REG, XO:XO + 32], oT_x[:, :], const[0:32, C_ID:C_ID + 32])
                mm.then_inc(out_turned, 1)

            def head(b, r, first, more):
                n = num(b, r)
                chunks = [(1, j) for j in range(AHEAD, NCH)] + [(2, j) for j in range(AHEAD)]

                def ahead(count):
                    for _ in range(count):
                        step, j = chunks.pop(0)
                        if step <= more:
                            max_scores(b, r + step, j)

                for kb in range(TPB):
                    ahead(BEFORE[kb][0])
                    exp_scores(b, r, kb)
                    if kb == 0 and extra is not None:
                        extra_scores(b, r)
                    if kb == 0:
                        ahead(BEFORE[0][1])
                        continue
                    if kb == 1 and not first:
                        values(b, r - 1, TPB - 1)
                    ahead(BEFORE[kb][1])
                    if kb == TURN and more:
                        turn_max(b, r + 1, n)
                    if kb == 1 and not first:
                        if extra is not None:
                            pe.wait_ge(xprobs_ready, n + 1)
                        turn_out(num(b, r - 1))
                    values(b, r, kb - 1)
                if not more:
                    values(b, r, TPB - 1)
                    pe.wait_ge(divided, n)
                    turn_out(n)

            pe.wait_ge(consts_set, 4)
            run = per_head(pe, head)
            for b in range(BATCH):
                for j in range(NCH):
                    max_scores(b, 0, j)
                turn_max(b, 0, b * HEADS)
                for j in range(AHEAD):
                    max_scores(b, 1, j)
                run(b)

        @block.vector
        def _(dve):
            def maxima(b, r, js):
                for j in js:
                    qt, c = CHUNKS[j]
                    tiles = min(4, qt + 1 - 4 * c) if causal else 4
                    dve.wait_ge(small_filled[j % 2], num(b, r) * HALF + (j // 2 + 1))
                    nc.vector.tensor_reduce(mxp[:, c, qt:qt + 1], small[j % 2][:, 0:tiles * P], AX.X,
                                            ALU.max).then_inc(small_used[j % 2], 1)

            def negated(b, r):
                n = num(b, r)
                for bank in range(2):
                    dve.wait_ge(small_used[bank], (n + 1) * HALF)
                nc.vector.tensor_tensor(mx[:, :], mxp[:, 0, :], mxp[:, 1, :], ALU.max).then_inc(mx_ready, 1)
                dve.wait_ge(mx_ready, n + 1)
                dve.wait_ge(rows_ready, n)
                nc.vector.tensor_scalar(negm[:, :, KM], mx[:, :], -1.0, None, ALU.mult).then_inc(hi_set, 1)
                dve.wait_ge(hi_set, n + 1)
                nc.vector.scalar_tensor_tensor(negm[:, :, KM + 1], mx[:, :], -1.0, negm[:, :, KM],
                                               ALU.mult, ALU.subtract).then_inc(negm_ready, 1)

            def divide(b, r):
                n = num(b, r)
                rows = turn_ps[:, 0:2 * P].rearrange("p (c g x) -> p c g x", c=2, x=32)
                rec3 = rec[:, :].rearrange("p (c g) -> p c g", c=2)
                dve.wait_ge(out_turned, n + 1)
                nc.vector.reciprocal(rec3.unsqueeze(3), rows[:, :, :, HD:HD + 1]).then_inc(rec_ready, 1)
                if extra is not None:
                    nc.vector.reciprocal(rec_x[:, :], turn_ps[0:REG, XO + HD:XO + HD + 1]).then_inc(rec_ready, 1)
                dve.wait_ge(rec_ready, (n + 1) * (1 if extra is None else 2))
                if extra is not None:
                    nc.vector.tensor_scalar(ctx_x[:, part(n, HD)], turn_ps[0:REG, XO:XO + HD],
                                            rec_x[:, 0:1], None, ALU.mult).then_inc(xdone, 1)
                dst = ctx_out[:, b * TPB * D:(b + 1) * TPB * D].rearrange("p (g c x) -> p c g x", g=G, c=2)
                nc.vector.tensor_tensor(dst[:, :, :, at(r * HD, HD)], rows[:, :, :, 0:HD],
                                        rec3.unsqueeze(3).broadcast_to([P, 2, G, HD]), ALU.mult).then_inc(divided, 1)

            def head(b, r, first, more):
                if more:
                    maxima(b, r + 1, range(AHEAD, AHEAD + 3))
                if not first:
                    divide(b, r - 1)
                if more:
                    maxima(b, r + 1, range(AHEAD + 3, NCH))
                    negated(b, r + 1)
                if more > 1:
                    maxima(b, r + 2, range(AHEAD))
                if not more:
                    dve.wait_ge(divided, num(b, r))
                    divide(b, r)

            nc.vector.tensor_copy(maskb[:, :], const[:, C_MASK:C_MASK + 2 * P]).then_inc(consts_set, 1)
            nc.vector.memset(mxp[:, :, :], -3e38).then_inc(consts_set, 1)
            nc.vector.memset(negm[:, :, :], 0.0).then_inc(consts_set, 1)
            nc.vector.memset(vst[:, :, :], 0.0).then_inc(consts_set, 1)
            dve.wait_ge(consts_set, 4)
            nc.vector.memset(vst[:, :, HD:HD + 1], 1.0).then_inc(ones_set, 1)
            run = per_head(dve, head)
            for b in range(BATCH):
                if extra is not None:
                    dve.wait_ge(rows_ready, b * HEADS)
                    nc.vector.tensor_copy(negm[:, :, KS:KS + 2], pen[:, b * TPB * 2:(b + 1) * TPB * 2].rearrange(
                        "p (t c) -> p t c", c=2)).then_inc(pen_set, 1)
                maxima(b, 0, range(NCH))
                negated(b, 0)
                maxima(b, 1, range(AHEAD))
                run(b)
            dve.wait_ge(divided, BATCH * HEADS)

        @block.scalar
        def _(act):
            def rows(b, r):
                act.wait_ge(max_turned, num(b, r) + 1)
                src = turn_ps[:, :].bitcast(BF16)[KS:KE, :].rearrange("p (t x) -> p t x", t=TPB)
                nc.scalar.copy(tiles_of(QT, slice(KS, KE), b, r, 0, TPB), src).then_inc(rows_ready, 1)

            def copy_sums(n):
                act.wait_ge(probs_used[1], (n + 1) * (TPB // 2))
                if extra is not None:
                    nc.scalar.copy(oT_x[:, :], out_ps[0:32, XO:XO + REG]).then_inc(oT_part, 1)
                    act.wait_ge(oT_part, n + 1)
                nc.scalar.copy(oT[:, :], out_ps[:, 0:2 * P]).then_inc(oT_ready, 1)

            def head(b, r, first, more):
                n = num(b, r)
                for kb in range(TPB):
                    w = kb % 2
                    cols = (TPB - kb if causal else TPB) * P
                    act.wait_ge(scores_ready[w], uses(n, kb) + 1)
                    act.wait_ge(probs_used[w], uses(n, kb))
                    nc.scalar.activation(probs[w][:, 0:cols], wide[w][:, 0:cols], ACT.Exp,
                                         scale=SCALE).then_inc(probs_ready[w], 1)
                    if kb == 0:
                        if extra is not None:
                            act.wait_ge(xscores_ready, n + 1)
                            act.wait_ge(xout_ready, n)
                            nc.scalar.activation(probs_x[:, :], turn_ps[:, 0:TPB * REG], ACT.Exp,
                                                 scale=SCALE).then_inc(xprobs_ready, 1)
                        if not first:
                            copy_sums(num(b, r - 1))
                    if kb == TURN and more:
                        rows(b, r + 1)
                if not more:
                    copy_sums(n)

            run = per_head(act, head)
            for b in range(BATCH):
                rows(b, 0)
                run(b)

        @block.gpsimd
        def _(pool):
            def stage(b, r):
                pool.wait_ge(probs_used[1], num(b, r) * (TPB // 2))
                src = V[:, b * TPB * D:(b + 1) * TPB * D].rearrange("p (t x) -> p t x", t=TPB)
                nc.gpsimd.tensor_copy(vst[:, :, 0:HD], src[:, :, at(r * HD, HD)]).then_inc(v_staged, 1)

            pool.wait_ge(ones_set, 1)
            for b in range(BATCH):
                stage(b, 0)
                with pool.Fori(1, HEADS) as r:
                    stage(b, r)


def project_out(nc, h, ctx_in, const, w_dram, name, bias_dram=None, out_dram=None):
    with ExitStack() as ctx:
        sb, ps, sem = scope(nc, ctx)
        w = sb(f"{name}_w", [P, 2, D], F32)
        stage = [sb(f"{name}_stage{i}", [P, D], F32) for i in range(2)]
        cT = [sb(f"{name}_cT{i}", [P, D], F32) for i in range(2)]
        cT_ps = [ps(f"{name}_cT_ps{i}", [P, D]) for i in range(2)]
        y_ps = [ps(f"{name}_y_ps{i}", [P, D]) for i in range(2)]
        w_in = sem("w_in")
        staged = [sem("staged0"), sem("staged1")]
        turned = [sem("turned0"), sem("turned1")]
        cT_ready = [sem("cT_ready0"), sem("cT_ready1")]
        y_ready = [sem("y_ready0"), sem("y_ready1")]
        added = [sem("added0"), sem("added1")]
        stored = sem("stored")
        NW = 16
        if bias_dram is not None:
            bias = sb(f"{name}_bias", [1, D], F32)
            NW = 32
        ident = const[:, C_ID:C_ID + P]
        block = ctx.enter_context(nc.Block())

        @block.sync
        def _(sp):
            sp.dma_start(w[:, :, :], w_dram.rearrange("(c p) n -> p c n", p=P)).then_inc(w_in, 16)
            if bias_dram is not None:
                sp.dma_start(bias[:, :], bias_dram.rearrange("(a n) -> a n", a=1)).then_inc(w_in, 16)
            if out_dram is not None:
                o3 = out_dram.rearrange("b (t p) d -> p (b t) d", p=P)
                h3 = h[:, :].rearrange("p (t d) -> p t d", d=D)
                for c in range(4):
                    for i in range(2):
                        sp.wait_ge(added[i], 2 * (c + 1))
                    sp.dma_start(o3[:, 4 * c:4 * c + 4, :], h3[:, 4 * c:4 * c + 4, :]).then_inc(stored, 16)
                sp.wait_ge(stored, 64)

        @block.gpsimd
        def _(pool):
            with pool.Fori(0, NT // 2) as s:
                for i in range(2):
                    pool.wait_ge(turned[i], s)
                    nc.gpsimd.tensor_copy(stage[i][:, :], ctx_in[:, at(s * 2 * D + i * D, D)]).then_inc(staged[i], 1)

        @block.tensor
        def _(pe):
            pe.wait_ge(w_in, NW)
            with pe.Fori(0, NT // 2) as s:
                for i in range(2):
                    pe.wait_ge(staged[i], s + 1)
                    pe.wait_ge(cT_ready[i], s)
                    for c in range(2):
                        mm = pe.transpose(cT_ps[i][:, c * P:(c + 1) * P], stage[i][:, c * P:(c + 1) * P], ident)
                    mm.then_inc(turned[i], 1)
                for i in range(2):
                    pe.wait_ge(cT_ready[i], s + 1)
                    pe.wait_ge(added[i], s)
                    for c in range(2):
                        mm = pe.matmul(y_ps[i][:, :], cT[i][:, c * P:(c + 1) * P], w[:, c, :],
                                       start=c == 0, stop=c == 1 and bias_dram is None)
                    if bias_dram is not None:
                        mm = pe.matmul(y_ps[i][:, :], const[0:1, C_ONES:C_ONES + P], bias[:, :], start=False, stop=True)
                    mm.then_inc(y_ready[i], 1)

        @block.scalar
        def _(act):
            with act.Fori(0, NT // 2) as s:
                for i in range(2):
                    act.wait_ge(turned[i], s + 1)
                    act.wait_ge(y_ready[i], s)
                    nc.scalar.copy(cT[i][:, :], cT_ps[i][:, :]).then_inc(cT_ready[i], 1)

        @block.vector
        def _(dve):
            with dve.Fori(0, NT // 2) as s:
                for i in range(2):
                    dve.wait_ge(y_ready[i], s + 1)
                    hs = h[:, at(s * 2 * D + i * D, D)]
                    nc.vector.tensor_tensor(hs, y_ps[i][:, :], hs, ALU.add).then_inc(added[i], 1)
            for i in range(2):
                dve.wait_ge(added[i], NT // 2)


def refined_root(dve, nc, root, x, tmp, done, base):
    nc.vector.reciprocal(tmp, root).then_inc(done, 1)
    dve.wait_ge(done, base + 1)
    nc.vector.tensor_tensor(tmp, tmp, x, ALU.mult).then_inc(done, 1)
    dve.wait_ge(done, base + 2)
    nc.vector.tensor_tensor(tmp, tmp, root, ALU.add).then_inc(done, 1)
    dve.wait_ge(done, base + 3)
    nc.vector.tensor_scalar(root, tmp, 0.5, None, ALU.mult).then_inc(done, 1)
    dve.wait_ge(done, base + 4)


def gauge_vector(nc, gq, g_dram):
    with ExitStack() as ctx:
        sb, ps, sem = scope(nc, ctx)
        sq = sb("gv_sq", [P, D], F32)
        n2 = sb("gv_n2", [P, HEADS], F32)
        root = sb("gv_root", [P, HEADS], F32)
        tmp = sb("gv_tmp", [P, HEADS], F32)
        g_in, step, n2_ready, root_ready = sem("g_in"), sem("step"), sem("n2_ready"), sem("root_ready")
        block = ctx.enter_context(nc.Block())

        @block.sync
        def _(sp):
            sp.dma_start(gq[:, :], g_dram[0, 0:1, :].broadcast_to([P, D])).then_inc(g_in, 16)
            sp.wait_ge(g_in, 16)

        @block.vector
        def _(dve):
            g3 = gq[:, :].rearrange("p (g d) -> p g d", d=HD)
            dve.wait_ge(g_in, 16)
            nc.vector.tensor_tensor(sq[:, :], gq[:, :], gq[:, :], ALU.mult).then_inc(step, 1)
            dve.wait_ge(step, 1)
            nc.vector.tensor_reduce(n2[:, :], sq[:, :].rearrange("p (g d) -> p g d", d=HD), AX.X,
                                    ALU.add).then_inc(n2_ready, 1)
            dve.wait_ge(root_ready, 1)
            refined_root(dve, nc, root[:, :], n2[:, :], tmp[:, :], step, 1)
            nc.vector.reciprocal(tmp[:, :], root[:, :]).then_inc(step, 1)
            dve.wait_ge(step, 6)
            nc.vector.tensor_tensor(g3, g3, tmp[:, :].unsqueeze(2).broadcast_to([P, HEADS, HD]),
                                    ALU.mult).then_inc(step, 1)
            dve.wait_ge(step, 7)

        @block.scalar
        def _(act):
            act.wait_ge(n2_ready, 1)
            nc.scalar.activation(root[:, :], n2[:, :], ACT.Sqrt).then_inc(root_ready, 1)


def group_tokens(nc, const, identb, gdot, gnorm, QT, KT, QX, pen):
    with ExitStack() as ctx:
        sb, ps, sem = scope(nc, ctx)
        NTH = NT * HEADS
        KM, KE = KS + 2, KS + 4
        RX = HEADS * REG
        root = sb("gt_root", [P, NTH], F32)
        tmp = sb("gt_tmp", [P, NTH], F32)
        sim = sb("gt_sim", [P, NT], F32)
        ends = sb("gt_ends", [P, 2, NT], F32)
        end1 = sb("gt_end1", [P, 2], F32)
        endall = sb("gt_endall", [P, 2], F32)
        width = sb("gt_width", [P, 2], F32)
        flag = sb("gt_flag", [P, NT], F32)
        qflag = sb("gt_qflag", [P, NT], F32)
        rows = sb("gt_rows", [P, 2, NT, KE], BF16)
        rowT = sb("gt_rowT", [KE, 2, NT * P], BF16)
        QZ = sb("gt_QZ", [KM, HEADS * (RX + REG)], BF16)
        zx = sb("gt_zx", [RX, BATCH, KE], BF16)
        mxx = sb("gt_mxx", [RX, BATCH], F32)
        row_ps = [ps(f"gt_row_ps{i}", [KE, TPB * P], BF16) for i in range(4)]
        x_ps = ps("gt_x_ps", [RX, SEQ])
        zx_ps = ps("gt_zx_ps", [KE, BATCH * RX], BF16)
        step, root_ready, ends_ready, ends_all, flags_ready = (
            sem("step"), sem("root_ready"), sem("ends_ready"), sem("ends_all"), sem("flags_ready"))
        rows_turned, rowT_ready, spread, zero, qz_ready, x_ready, zx_ready, zx_turned = (
            sem("rows_turned"), sem("rowT_ready"), sem("spread"), sem("zero"), sem("qz_ready"), sem("x_ready"),
            sem("zx_ready"), sem("zx_turned"))
        token = const[:, C_TOKM:C_TOKM + NT]
        block = ctx.enter_context(nc.Block())

        @block.scalar
        def _(act):
            nc.scalar.activation(root[:, :], gnorm[:, :], ACT.Sqrt).then_inc(root_ready, 1)
            for i in range(4):
                act.wait_ge(rows_turned, i + 1)
                nc.scalar.copy(rowT[KS:KS + 2, i // 2, (i % 2) * TPB * P:(i % 2 + 1) * TPB * P],
                               row_ps[i][KS:KS + 2, :]).then_inc(rowT_ready, 1)

        @block.vector
        def _(dve):
            n = 0

            def then(ins):
                nonlocal n
                n += 1
                ins.then_inc(step, 1)
                dve.wait_ge(step, n)

            nc.vector.memset(rows[:, :, :, :], 0.0).then_inc(zero, 1)
            nc.vector.memset(QZ[:, :], 0.0).then_inc(zero, 1)
            nc.vector.memset(zx[:, :, :], 0.0).then_inc(zero, 1)
            dve.wait_ge(root_ready, 1)
            refined_root(dve, nc, root[:, :], gnorm[:, :], tmp[:, :], step, 0)
            n = 4
            then(nc.vector.reciprocal(tmp[:, :], root[:, :]))
            then(nc.vector.tensor_tensor(tmp[:, :], gdot[:, :], tmp[:, :], ALU.mult))
            then(nc.vector.tensor_reduce(sim[:, :], tmp[:, :].rearrange("p (t g) -> p t g", g=HEADS), AX.X, ALU.add))
            then(nc.vector.tensor_scalar(sim[:, :], sim[:, :], 1.0 / HEADS, None, ALU.mult))
            then(nc.vector.tensor_tensor(ends[:, 0, :], sim[:, :], const[:, C_REG:C_REG + NT], ALU.add))
            then(nc.vector.scalar_tensor_tensor(ends[:, 1, :], sim[:, :], -1.0, const[:, C_REG:C_REG + NT],
                                                ALU.mult, ALU.add))
            nc.vector.tensor_reduce(end1[:, :], ends[:, :, :], AX.X, ALU.max).then_inc(ends_ready, 1)
            dve.wait_ge(ends_all, 1)
            then(nc.vector.tensor_tensor(width[:, 0:1], endall[:, 0:1], endall[:, 1:2], ALU.add))
            then(nc.vector.reciprocal(width[:, 1:2], width[:, 0:1]))
            then(nc.vector.tensor_scalar(sim[:, :], sim[:, :], endall[:, 1:2], width[:, 1:2], ALU.add, ALU.mult))
            then(nc.vector.tensor_scalar(flag[:, :], sim[:, :], 0.9, None, ALU.is_gt))
            dve.wait_ge(zero, 3)
            then(nc.vector.tensor_tensor(flag[:, :], flag[:, :], token, ALU.mult))
            then(nc.vector.tensor_copy(rows[:, 0, :, KS], flag[:, :]))
            then(nc.vector.tensor_tensor(rows[:, 0, :, KS + 1], token, flag[:, :], ALU.subtract))
            then(nc.vector.tensor_tensor(qflag[:, :], flag[:, :], token, ALU.subtract))
            then(nc.vector.tensor_scalar(qflag[:, :], qflag[:, :], 1.0, None, ALU.add))
            p3 = pen[:, :].rearrange("p (t c) -> p t c", c=2)
            then(nc.vector.tensor_scalar(p3[:, :, 0], qflag[:, :], -NEG, NEG, ALU.mult, ALU.add))
            then(nc.vector.tensor_scalar(p3[:, :, 1], qflag[:, :], NEG, None, ALU.mult))
            nc.vector.tensor_copy(rows[:, 1, :, KS:KS + 2], p3).then_inc(flags_ready, 1)
            for b in range(BATCH):
                src = QT[0:KS, b * TPB * HEADS * P:(b * TPB + 1) * HEADS * P].rearrange("p (g x) -> p g x", g=HEADS)
                then(nc.vector.tensor_copy(QX[0:KS, b * RX:(b + 1) * RX].rearrange("p (g r) -> p g r", r=REG),
                                           src[:, :, 0:REG]))
            for b in range(BATCH):
                dve.wait_ge(x_ready, b)
                qz = QZ[0:KS, :].rearrange("p (g x) -> p g x", x=RX + REG)
                then(nc.vector.tensor_copy(qz[:, :, 0:REG], QX[0:KS, b * RX:(b + 1) * RX].rearrange(
                    "p (g r) -> p g r", r=REG)))
                nc.vector.memset(QZ[KS:KS + 1, :].rearrange("p (g x) -> p g x", x=RX + REG)[:, :, 0:REG],
                                 NEG).then_inc(qz_ready, 1)
                dve.wait_ge(x_ready, b + 1)
                then(nc.vector.tensor_reduce(mxx[:, b:b + 1], x_ps[:, :], AX.X, ALU.max))
                then(nc.vector.memset(zx[:, b, KS:KS + 1], NEG))
                then(nc.vector.tensor_scalar(zx[:, b, KM:KM + 1], mxx[:, b:b + 1], -1.0, None, ALU.mult))
                nc.vector.scalar_tensor_tensor(zx[:, b, KM + 1:KM + 2], mxx[:, b:b + 1], -1.0,
                                               zx[:, b, KM:KM + 1], ALU.mult, ALU.subtract).then_inc(zx_ready, 1)
            dve.wait_ge(zx_turned, 1)
            then(nc.vector.tensor_copy(QX[KS:KE, :], zx_ps[KS:KE, :]))

        @block.gpsimd
        def _(pool):
            pool.wait_ge(ends_ready, 1)
            nc.gpsimd.partition_all_reduce(endall[:, :], end1[:, :], P, bass.bass_isa.ReduceOp.max).then_inc(ends_all, 1)

        @block.tensor
        def _(pe):
            pe.wait_ge(flags_ready, 1)
            for i in range(4):
                for t in range(TPB):
                    mm = pe.transpose(row_ps[i][:, t * P:(t + 1) * P], rows[:, i // 2, (i % 2) * TPB + t, :],
                                      identb[:, :])
                mm.then_inc(rows_turned, 1)
            pe.wait_ge(spread, 64 * TPB)
            for b in range(BATCH):
                pe.wait_ge(qz_ready, b + 1)
                pe.wait_ge(zx_ready, b)

                def scores(g):
                    for c in range(2):
                        k3 = KT[0:KM, (b * TPB + 4 * c) * HEADS * P:(b * TPB + 4 * c + 4) * HEADS * P].rearrange(
                            "p (t x) -> p t x", t=4)
                        mm = pe.matmul(x_ps[:, c * 512:(c + 1) * 512].rearrange("p (t x) -> p t x", t=4),
                                       QZ[:, at(g * RX, RX)], k3[:, :, at(g * P, P)],
                                       start=isinstance(g, int) and g == 0, stop=isinstance(g, int) and g > 0,
                                       skip_group_check=True)
                    return mm

                scores(0)
                with pe.Fori(1, HEADS - 1) as g:
                    scores(g)
                scores(HEADS - 1).then_inc(x_ready, 1)
            pe.wait_ge(zx_ready, BATCH)
            for b in range(BATCH):
                mm = pe.transpose(zx_ps[:, b * RX:(b + 1) * RX], zx[:, b, :], identb[0:RX, 0:RX])
            mm.then_inc(zx_turned, 1)

        @block.sync
        def _(sp):
            for i in range(4):
                sp.wait_ge(rowT_ready, i + 1)
                b = i % 2
                dst = (KT, QT)[i // 2][KS:KS + 2, b * TPB * HEADS * P:(b + 1) * TPB * HEADS * P].rearrange(
                    "p (t g x) -> p t g x", t=TPB, g=HEADS)
                src = rowT[KS:KS + 2, i // 2, b * TPB * P:(b + 1) * TPB * P].rearrange("p (t x) -> p t x", t=TPB)
                for t in range(TPB):
                    sp.dma_start(dst[:, t], src[:, t].unsqueeze(1).broadcast_to([2, HEADS, P])).then_inc(spread, 16)
            sp.wait_ge(spread, 64 * TPB)


def merge_registers(nc, C, CX):
    with ExitStack() as ctx:
        sb, ps, sem = scope(nc, ctx)
        step = sem("step")
        block = ctx.enter_context(nc.Block())

        @block.vector
        def _(dve):
            for b in range(BATCH):
                rows = C[0:REG, b * TPB * D:b * TPB * D + D]
                nc.vector.tensor_tensor(rows, rows, CX[:, b * D:(b + 1) * D], ALU.add).then_inc(step, 1)
                dve.wait_ge(step, 2 * b + 1)
                nc.vector.tensor_scalar(rows, rows, 0.5, None, ALU.mult).then_inc(step, 1)
                dve.wait_ge(step, 2 * b + 2)


def mixture(nc, h, mean, rstd, const, T, x_scr, y_scr):
    with ExitStack() as ctx:
        sb, ps, sem = scope(nc, ctx)
        HG = GRP // 2
        NG = P // GRP
        CHO = 11
        aT_up = sb("aT_up", [P, E * F1], F32)
        bT_up = sb("bT_up", [P, E * F1], F32)
        aT_dn = sb("aT_dn", [P, E * D1], F32)
        bT_dn = sb("bT_dn", [P, E * D1], F32)
        wr_up = sb("wr_up", [P, 2 * SPM, E], F32)
        wr_dn = sb("wr_dn", [P, F1, E], F32)
        bias_up = sb("bias_up_sb", [F1, F1], F32)
        bias_dn = sb("bias_dn_sb", [D1, D1], F32)
        scales = sb("scales", [F1, 2], F32)
        X = sb("X", [D1, P * D1], F32)
        hid = sb("hid", [P, P * F1], F32)
        yo = sb("yo", [D1, P * D1], F32)
        lo_up = sb("lo_up", [P, NMT * E], F32)
        lo_dnT = sb("lo_dnT", [E, P], F32)
        scores = sb("scores", [P, E], F32)
        vals = sb("vals", [P, 8], F32)
        idx = sb("idx", [P, 8], U32)
        pr = sb("pr", [P, 8], F32)
        dg = sb("dg", [P, 4 * P], F32)
        weight = sb("weight", [F1, P * TOPK], F32)
        offset = sb("offset", [1, P * TOPK], I32)
        xs = [sb(f"xs{i}", [P, HG * D1], F32) for i in range(2)]
        hs = [sb(f"hs{i}", [P, HG * F1], F32) for i in range(2)]
        ts_up = [sb(f"ts_up{i}", [P, HG * TOPK * F1], F32) for i in range(2)]
        ts_dn = [sb(f"ts_dn{i}", [P, HG * TOPK * D1], F32) for i in range(2)]
        pre = [sb(f"pre{i}", [F1, HG * F1], F32) for i in range(2)]
        t_ps = [ps(f"t_ps{i}", [F1, HG * TOPK * F1]) for i in range(2)]
        y_ps = [ps(f"y_ps{i}", [F1, HG * F1]) for i in range(2)]
        r_ps = ps("r_ps", [P, 512])
        b_ps = ps("b_ps", [F1, 4 * P])
        ident = const[:, C_ID:C_ID + P]
        ones = const[:, C_ONES:C_ONES + F1]

        tabs_in, padded = sem("tabs_in"), sem("padded")
        load_tables = [
            (aT_up[0:D1, :], T["up_A"]), (bT_up[0:D1, :], T["up_B"]), (aT_dn[0:F1, :], T["dn_A"]), (bT_dn[0:F1, :], T["dn_B"]),
            (wr_up[:, :, :], T["up_W"].rearrange("(c p) e -> p c e", p=P)),
            (wr_dn[0:F1, :, :], T["dn_W"].rearrange("(o q) e -> o q e", o=F1)),
            (bias_up[:, :], T["up_bias"].rearrange("(o q) -> o q", o=F1)),
            (bias_dn[:, :], T["dn_bias"].rearrange("(o q) -> o q", o=D1)),
            (scales[:, 0:1], T["up_scale"].rearrange("(a b) -> a b", a=1).broadcast_to([F1, 1])),
            (scales[:, 1:2], T["dn_scale"].rearrange("(a b) -> a b", a=1).broadcast_to([F1, 1])),
        ]

        TABS = 16 * len(load_tables)

        with ExitStack() as part1:
            def sb1(name, shape, dt):
                return part1.enter_context(nc.sbuf_tensor(name, shape, dt))

            def ps1(name, shape, dt=F32):
                return part1.enter_context(nc.psum_tensor(name, shape, dt))

            def sem1(name):
                return part1.enter_context(nc.semaphore(name))

            xn = [sb1(f"m_xn{i}", [P, D], F32) for i in range(4)]
            xT = sb1("m_xT", [P, 2, 4 * P], F32)
            xT_ps = [ps1(f"m_xT_ps{i}", [P, D]) for i in range(2)]
            xT_ready = [sem1("xT_ready0"), sem1("xT_ready1")]
            xn_ready, xn_out, turned, logits_ready, logits_out = (
                sem1("xn_ready"), sem1("xn_out"), sem1("turned"), sem1("logits_ready"),
                sem1("logits_out"))
            block = part1.enter_context(nc.Block())

            @block.sync
            def _(sp):
                for dst, src in load_tables:
                    sp.dma_start(dst, src).then_inc(tabs_in, 16)
                with sp.Fori(0, NMT) as m:
                    for i in range(4):
                        sp.wait_ge(xn_ready, m * 4 + (i + 1))
                        sp.dma_start(x_scr[at(m * 4 * P + i * P, P), :], xn[i][:, :]).then_inc(xn_out, 16)
                sp.wait_ge(xn_out, 16 * NT)
                sp.wait_ge(tabs_in, TABS)

            @block.gpsimd
            def _(pool):
                low = ([(x, D1) for x in (aT_up, bT_up, *xs, *ts_up)]
                       + [(x, F1) for x in (aT_dn, bT_dn, wr_dn.rearrange("p q e -> p (q e)"), hid, *hs, *ts_dn)])
                spans = [(x, a, b) for x, rows in low for a, b in ((D1, F1), (F1, P)) if a >= rows]
                for x, a, b in spans:
                    nc.gpsimd.memset(x[a:b, :], 0.0).then_inc(padded, 1)
                pool.wait_ge(padded, len(spans))

            @block.vector
            def _(dve):
                with dve.Fori(0, NMT) as m:
                    for i in range(4):
                        dve.wait_ge(xn_out, (m * 4 + i) * 16)
                        dve.wait_ge(turned, m * 4 + i)
                        nc.vector.tensor_scalar(xn[i][:, :], h[:, at(m * 4 * D + i * D, D)],
                                                mean[:, at(m * 4 + i, 1)], rstd[:, at(m * 4 + i, 1)],
                                                ALU.subtract, ALU.mult).then_inc(xn_ready, 1)
                dve.wait_ge(xn_ready, NT)

            @block.tensor
            def _(pe):
                pe.wait_ge(tabs_in, TABS)
                with pe.Fori(0, NMT) as m:
                    for i in range(4):
                        pe.wait_ge(xn_ready, m * 4 + (i + 1))
                        pe.wait_ge(xT_ready[i % 2], m * 2 + i // 2)
                        for c in range(2):
                            mm = pe.transpose(xT_ps[i % 2][:, c * P:(c + 1) * P], xn[i][:, c * P:(c + 1) * P], ident)
                        mm.then_inc(turned, 1)
                    for i in range(2):
                        pe.wait_ge(xT_ready[i], m * 2 + 2)
                    pe.wait_ge(logits_out, m)
                    for s in range(SPM):
                        for c in range(2):
                            mm = pe.matmul(r_ps[:, 0:E], xT[:, c, s:4 * P:SPM], wr_up[:, 2 * s + c, :],
                                           start=s + c == 0, stop=s + c == SPM)
                    mm.then_inc(logits_ready, 1)

            @block.scalar
            def _(act):
                with act.Fori(0, NMT) as m:
                    for i in range(4):
                        act.wait_ge(turned, m * 4 + (i + 1))
                        act.wait_ge(logits_ready, m)
                        nc.scalar.copy(xT[:, :, i * P:(i + 1) * P],
                                       xT_ps[i % 2][:, :].rearrange("p (c x) -> p c x", c=2)).then_inc(xT_ready[i % 2], 1)
                    act.wait_ge(logits_ready, m + 1)
                    nc.scalar.copy(lo_up[:, part(m, E)], r_ps[:, 0:E]).then_inc(logits_out, 1)
                act.wait_ge(logits_out, NMT)

        step, diag_ready, spread, offset_ready, gap_ready, gap_exp = (
            sem("step"), sem("diag_ready"), sem("spread"), sem("offset_ready"), sem("gap_ready"), sem("gap_exp"))
        x_in = sem("x_in")
        waited, waited_pe = sem("waited"), sem("waited_pe")
        staged = [sem("staged0"), sem("staged1")]
        t_ready = [sem("t_ready0"), sem("t_ready1")]
        ts_ready = [sem("ts_ready0"), sem("ts_ready1")]
        y_ready = [sem("y_ready0"), sem("y_ready1")]
        y_read = [sem("y_read0"), sem("y_read1")]
        gelu_done, dn_scores, dn_copied, dn_logits, choice_read, yo_out = (
            [sem("gelu_done0"), sem("gelu_done1")], sem("dn_scores"), sem("dn_copied"), sem("dn_logits"), sem("choice_read"), sem("yo_out"))
        block = ctx.enter_context(nc.Block())

        def number(m, u, g):
            return m * (2 * NG) + (g + u * NG)

        @block.gpsimd
        def _(pool):
            with pool.Fori(0, NMT) as m:
                for u in range(2):
                    with pool.Fori(0, NG) as g:
                        for i in range(2):
                            n = number(m, u, g)
                            pool.wait_ge(t_ready[i], n)
                            if u == 0:
                                pool.wait_ge(x_in, m * 16 + 16)
                                nc.gpsimd.tensor_copy(xs[i][0:D1, :], X[:, at(g * GRP * D1 + i * HG * D1, HG * D1)]
                                                      ).then_inc(staged[i], 1)
                            else:
                                pool.wait_ge(gelu_done[i], m * NG + g + 1)
                                nc.gpsimd.tensor_copy(hs[i][0:F1, :], hid[0:F1, at(g * GRP * F1 + i * HG * F1, HG * F1)]
                                                      ).then_inc(staged[i], 1)

        @block.tensor
        def _(pe):
            def spread_choice(c):
                pe.wait_ge(diag_ready, c + 1)
                pe.wait_ge(offset_ready, c)
                pe.matmul(b_ps[:, :], ones, dg[:, :], start=True, stop=True).then_inc(spread, 1)

            def experts(m, u, g):
                n = number(m, u, g)
                N1, N2 = (F1, F1) if u == 0 else (D1, D1)
                ta, tb = (aT_up, bT_up) if u == 0 else (aT_dn, bT_dn)
                side = D1 if u == 0 else F1
                stage, ts = (xs, ts_up) if u == 0 else (hs, ts_dn)
                ROWS = D1 if u == 0 else F1
                _, offs = nc.values_load_multi_w_load_instructions(
                    offset[0:1, at(g * GRP * TOPK, GRP * TOPK)], engines=[mybir.EngineType.PE], min_val=0,
                    max_val=(E - 1) * N1, skip_runtime_bounds_check_because="max_index returns 0 to E - 1")
                for i in range(2):
                    pe.wait_ge(staged[i], n + 1)
                    pe.wait_ge(ts_ready[i], n)
                    for q in range(HG):
                        for k in range(TOPK):
                            j = q * TOPK + k
                            mm = pe.matmul(t_ps[i][0:ROWS, j * N1:(j + 1) * N1], stage[i][:, q * side:(q + 1) * side],
                                           ta[:, at(offs[i * HG * TOPK + j], N1)], start=True, stop=True)
                    mm.then_inc(t_ready[i], 1)
                for i in range(2):
                    pe.wait_ge(ts_ready[i], n + 1)
                    pe.wait_ge(y_read[i], n)
                    for q in range(HG):
                        for k in range(TOPK):
                            j = q * TOPK + k
                            mm = pe.matmul(y_ps[i][0:N1, q * N2:(q + 1) * N2], ts[i][:, j * N1:(j + 1) * N1],
                                           tb[:, at(offs[i * HG * TOPK + j], N2)], start=k == 0, stop=k == TOPK - 1)
                    mm.then_inc(y_ready[i], 1)

            with pe.Fori(0, NMT) as m:
                for u in range(2):
                    if u == 1:
                        for i in range(2):
                            pe.wait_ge(gelu_done[i], m * NG + NG)
                        pe.wait_ge(choice_read, m * 4)
                        h3 = hid[:, :].rearrange("p (n q) -> p n q", q=F1)
                        for q in range(F1):
                            mm = pe.matmul(r_ps[0:E, 0:P], wr_dn[:, q, :], h3[:, :, q], start=q == 0, stop=q == F1 - 1)
                        mm.then_inc(dn_scores, 1)
                        pe.wait_ge(dn_copied, m + 1)
                        pe.sem_inc(waited_pe, 1)
                        pe.transpose(r_ps[:, P:P + E], lo_dnT[:, :], const[0:E, C_ID:C_ID + E]).then_inc(dn_logits, 1)
                    spread_choice(m * 2 + u)
                    pe.wait_ge(offset_ready, m * 2 + (u + 1))
                    pe.sem_inc(waited_pe, 1)
                    with pe.Fori(0, NG) as g:
                        experts(m, u, g)

        @block.vector
        def _(dve):
            def choose_two(m, u):
                c = m * 2 + u
                if u == 0:
                    logits = lo_up[:, part(m, E)]
                else:
                    dve.wait_ge(dn_scores, m + 1)
                    nc.vector.tensor_copy(lo_dnT[:, :], r_ps[0:E, 0:P]).then_inc(dn_copied, 1)
                    dve.wait_ge(dn_logits, m + 1)
                    logits = r_ps[:, P:P + E]
                base = [c * CHO]

                def then(ins):
                    base[0] = base[0] + 1
                    ins.then_inc(step, 1)
                    dve.wait_ge(step, base[0])

                nc.vector.tensor_copy(scores[:, :], logits).then_inc(choice_read, 1)
                dve.wait_ge(choice_read, c * 2 + 1)
                dve.sem_inc(waited, 1)
                then(nc.vector.max(out=vals[:, :], in_=scores[:, :]))
                dve.sem_inc(waited, 1)
                nc.vector.max_index(out=idx[:, :], in_max=vals[:, :], in_values=scores[:, :]).then_inc(choice_read, 1)
                dve.wait_ge(choice_read, c * 2 + 2)
                nc.vector.tensor_tensor(pr[:, 0:1], vals[:, 1:2], vals[:, 0:1], ALU.subtract).then_inc(gap_ready, 1)
                then(nc.vector.tensor_copy(pr[:, 4:6], idx[:, 0:2]))
                dve.wait_ge(gap_exp, c + 1)
                then(nc.vector.tensor_scalar(pr[:, 2:3], pr[:, 1:2], 1.0, None, ALU.add))
                then(nc.vector.reciprocal(pr[:, 2:3], pr[:, 2:3]))
                then(nc.vector.tensor_tensor(pr[:, 3:4], pr[:, 1:2], pr[:, 2:3], ALU.mult))
                dve.wait_ge(spread, c)
                for k in range(2):
                    then(nc.vector.tensor_scalar(dg[:, k * P:(k + 1) * P], ident, pr[:, 2 + k:3 + k], None, ALU.mult))
                for k in range(2):
                    then(nc.vector.tensor_scalar(dg[:, (2 + k) * P:(3 + k) * P], ident, pr[:, 4 + k:5 + k],
                                                 None, ALU.mult))
                dve.sem_inc(diag_ready, 1)
                dve.wait_ge(spread, c + 1)
                b3 = b_ps[:, :].rearrange("p (k n) -> p n k", k=4)
                then(nc.vector.tensor_copy(weight[:, :].rearrange("p (n k) -> p n k", k=TOPK), b3[:, :, 0:TOPK]))
                then(nc.vector.tensor_scalar(offset[:, :].rearrange("p (n k) -> p n k", k=TOPK), b3[0:1, :, TOPK:2 * TOPK],
                                             float(F1 if u == 0 else D1), None, ALU.mult))
                dve.sem_inc(offset_ready, 1)

            def weigh(m, u, g, i):
                n = number(m, u, g)
                ROWS, N1, ts = (D1, F1, ts_up) if u == 0 else (F1, D1, ts_dn)
                W = HG * TOPK
                dve.wait_ge(t_ready[i], n + 1)
                dve.wait_ge(y_ready[i], n)
                nc.vector.tensor_tensor(
                    ts[i][0:ROWS, 0:W * N1].rearrange("p (j x) -> p j x", j=W),
                    t_ps[i][0:ROWS, 0:W * N1].rearrange("p (j x) -> p j x", j=W),
                    weight[0:ROWS, at(g * GRP * TOPK + i * W, W)].unsqueeze(2).broadcast_to([ROWS, W, N1]),
                    ALU.mult).then_inc(ts_ready[i], 1)

            def result(m, u, g, i):
                n = number(m, u, g)
                dve.wait_ge(y_ready[i], n + 1)
                if u == 0:
                    dve.wait_ge(gelu_done[i], m * NG + g)
                    nc.vector.scalar_tensor_tensor(
                        pre[i][:, :].rearrange("p (n x) -> p n x", x=F1), y_ps[i][:, :].rearrange("p (n x) -> p n x", x=F1),
                        scales[:, 0:1], bias_up[:, :].unsqueeze(1).broadcast_to([F1, HG, F1]),
                        ALU.mult, ALU.add).then_inc(y_read[i], 1)
                else:
                    nc.vector.scalar_tensor_tensor(
                        yo[:, at(g * GRP * D1 + i * HG * D1, HG * D1)].rearrange("p (n x) -> p n x", x=D1),
                        y_ps[i][0:D1, 0:HG * D1].rearrange("p (n x) -> p n x", x=D1),
                        scales[0:D1, 1:2], bias_dn[:, :].unsqueeze(1).broadcast_to([D1, HG, D1]),
                        ALU.mult, ALU.add).then_inc(y_read[i], 1)

            with dve.Fori(0, NMT) as m:
                for u in range(2):
                    choose_two(m, u)
                    if u == 1:
                        dve.wait_ge(yo_out, m * 16)
                        dve.sem_inc(waited, 1)
                    with dve.Fori(0, NG) as g:
                        for i in range(2):
                            weigh(m, u, g, i)
                        for i in range(2):
                            result(m, u, g, i)

        @block.scalar
        def _(act):
            def gap(c):
                act.wait_ge(gap_ready, c + 1)
                nc.scalar.activation(pr[:, 1:2], pr[:, 0:1], ACT.Exp).then_inc(gap_exp, 1)

            with act.Fori(0, NMT) as m:
                gap(m * 2)
                with act.Fori(0, NG) as g:
                    for i in range(2):
                        n = number(m, 0, g)
                        act.wait_ge(y_read[i], n + 1)
                        act.wait_ge(t_ready[i], n)
                        nc.scalar.activation(hid[0:F1, at(g * GRP * F1 + i * HG * F1, HG * F1)], pre[i][:, :],
                                             ACT.Gelu).then_inc(gelu_done[i], 1)
                gap(m * 2 + 1)

        @block.sync
        def _(sp):
            y3 = y_scr.rearrange("(n s) f -> n (s f)", s=SPM)
            x3 = x_scr.rearrange("(n s) f -> n (s f)", s=SPM)

            def load(m):
                sp.dma_start(X[:, :].rearrange("i (n j) -> i n j", j=D1),
                             x3[at(m * P, P), :].rearrange("n (i j) -> i n j", j=D1)).then_inc(x_in, 16)

            def store(m):
                for i in range(2):
                    sp.wait_ge(y_read[i], m * (2 * NG) + 2 * NG)
                sp.dma_start(y3[at(m * P, P), :].rearrange("n (o q) -> o n q", q=D1),
                             yo[:, :].rearrange("p (n x) -> p n x", x=D1)).then_inc(yo_out, 16)

            load(0)
            with sp.Fori(0, NMT - 1) as m:
                for i in range(2):
                    sp.wait_ge(staged[i], m * (2 * NG) + NG)
                load(m + 1)
                store(m)
            store(NMT - 1)
            sp.wait_ge(yo_out, 16 * NMT)


def add_mixture(nc, h, y_scr, out_dram=None):
    with ExitStack() as ctx:
        sb, ps, sem = scope(nc, ctx)
        y = sb("am_y", [P, NT * D], F32)
        y_in, added, stored = [sem(f"y_in{c}") for c in range(4)], sem("added"), sem("stored")
        block = ctx.enter_context(nc.Block())

        @block.sync
        def _(sp):
            for c in range(4):
                sp.dma_start(y[:, part(c, 4 * D)].rearrange("p (t d) -> p t d", d=D),
                             y_scr[part(c, 4 * P), :].rearrange("(t p) d -> p t d", p=P)).then_inc(y_in[c], 16)
            for c in range(4):
                sp.wait_ge(y_in[c], 16)
            if out_dram is not None:
                sp.wait_ge(added, 4)
                sp.dma_start(out_dram.rearrange("b (t p) d -> p (b t) d", p=P),
                             h[:, :].rearrange("p (t d) -> p t d", d=D)).then_inc(stored, 16)
                sp.wait_ge(stored, 16)

        @block.vector
        def _(dve):
            for c in range(4):
                dve.wait_ge(y_in[c], 16)
                hs = h[:, part(c, 4 * D)]
                nc.vector.tensor_tensor(hs, hs, y[:, part(c, 4 * D)], ALU.add).then_inc(added, 1)
            dve.wait_ge(added, 4)


def tower(nc, T, out, upto=99):
    with ExitStack() as ctx:
        def sb(name, shape, dt):
            return ctx.enter_context(nc.sbuf_tensor(name, shape, dt))

        h = sb("h", [P, NT * D], F32)
        const = sb("const_sb", [P, C_W], F32)
        identb = sb("identb", [P, P], BF16)
        ids = sb("ids_sb", [P, NT], I32)
        mean = sb("mean", [P, NT], F32)
        rstd = sb("rstd", [P, NT], F32)
        rows_in = ctx.enter_context(nc.semaphore("rows_in"))
        x_scr = nc.dram_tensor("x_scr", (TOK, D), F32, kind="Internal").ap()
        y_scr = nc.dram_tensor("y_scr", (TOK, D), F32, kind="Internal").ap()

        def attention(n, grouped=False, out_dram=None):
            with ExitStack() as layer:
                def lsb(name, shape, dt):
                    return layer.enter_context(nc.sbuf_tensor(f"L{n}_{name}", shape, dt))
                QT = lsb("QT", [KS + 4, NT * HEADS * P], BF16)
                KT = lsb("KT", [KS + 4, NT * HEADS * P], BF16)
                V = lsb("V", [P, NT * D], F32)
                if n == 0:
                    embed(nc, h, const, identb, ids, rows_in, T["ids"], T["tok_W"], T["const"])
                gauge = extra = None
                if grouped:
                    CX = lsb("CX", [REG, BATCH * D], F32)
                    QX = lsb("QX", [KS + 4, BATCH * HEADS * REG], BF16)
                    pen = lsb("pen", [P, NT * 2], BF16)
                    with ExitStack() as g:
                        gq = g.enter_context(nc.sbuf_tensor("gq", [P, D], F32))
                        gdot = g.enter_context(nc.sbuf_tensor("gdot", [P, NT * HEADS], F32))
                        gnorm = g.enter_context(nc.sbuf_tensor("gnorm", [P, NT * HEADS], F32))
                        gauge_vector(nc, gq, T["g_info"])
                        statistics(nc, h, mean, rstd, f"L{n}s")
                        project(nc, h, mean, rstd, const, identb, T[f"L{n}_Wqk"], T[f"L{n}_Wv"], QT, KT, V, False,
                                f"L{n}p", (gq, gdot, gnorm))
                        group_tokens(nc, const, identb, gdot, gnorm, QT, KT, QX, pen)
                    extra = (QX, CX, pen)
                else:
                    statistics(nc, h, mean, rstd, f"L{n}s")
                    project(nc, h, mean, rstd, const, identb, T[f"L{n}_Wqk"], T[f"L{n}_Wv"], QT, KT, V, True, f"L{n}p")
                C = lsb("C", [P, NT * D], F32)
                attend(nc, const, identb, QT, KT, V, C, not grouped, f"L{n}a", extra)
                if grouped:
                    merge_registers(nc, C, CX)
                project_out(nc, h, C, const, T[f"L{n}_Wo"], f"L{n}o", T["L2_bias"] if grouped else None, out_dram)

        attention(0, out_dram=out if upto == 1 else None)
        if upto == 1:
            return
        statistics(nc, h, mean, rstd, "Ms")
        mixture(nc, h, mean, rstd, const, T, x_scr, y_scr)
        add_mixture(nc, h, y_scr, out if upto == 2 else None)
        if upto == 2:
            return
        recycle(nc)
        attention(1, out_dram=out if upto == 3 else None)
        if upto == 3:
            return
        recycle(nc)
        attention(2, True, out)


INPUTS = {
    "ids": ((P, NT), I32), "tok_W": ((50257, D), F32), "const": ((P, C_W), F32),
    **{f"L{n}_{w}": ((D, QK if w == "Wqk" else D), F32) for n in range(3) for w in ("Wqk", "Wv", "Wo")},
    "L2_bias": ((D,), F32), "g_info": ((12, 2, D), F32),
    "up_A": ((D1, E * F1), F32), "up_B": ((D1, E * F1), F32), "dn_A": ((F1, E * D1), F32), "dn_B": ((F1, E * D1), F32),
    "up_W": ((D1 * D1, E), F32), "dn_W": ((F1 * F1, E), F32), "up_bias": ((F1 * F1,), F32), "dn_bias": ((D1 * D1,), F32),
    "up_scale": ((1,), F32), "dn_scale": ((1,), F32),
}


def constants():
    import numpy as np
    c = np.zeros((P, C_W), np.float32)
    i = np.arange(P)
    c[:, C_ID:C_ID + P] = np.eye(P)
    c[:, C_MASK:C_MASK + P] = np.where(i[None, :] > i[:, None], NEG, 0)
    c[:, C_MASKT:C_MASKT + P] = np.where(i[None, :] < i[:, None], NEG, 0)
    inv = np.float32(1.0) / np.float32(10000.0) ** (np.arange(0, HD, 2, dtype=np.float32) / np.float32(HD))
    ang = np.arange(SEQ, dtype=np.float32)[:, None] * inv.astype(np.float32)[None, :]
    cos = np.repeat(np.cos(ang), 2, axis=1)
    sin = np.stack([-np.sin(ang), np.sin(ang)], axis=-1).reshape(SEQ, HD)
    for base, table in ((C_COS, cos), (C_SIN, sin)):
        c[:, base:base + TPB * HD] = table.reshape(TPB, P, HD).transpose(1, 0, 2).reshape(P, TPB * HD)
    reg = np.zeros((P, NT), bool)
    reg[0:REG, ::TPB] = True
    c[:, C_REG:C_REG + NT] = np.where(reg, NEG, 0)
    c[:, C_TOKM:C_TOKM + NT] = ~reg
    c[:, C_ONES:C_ONES + P] = 1.0
    return c


def kernel(**inputs):
    import numpy as _np
    import concourse.bacc as _bacc
    from concourse.bass_utils import run_bass_kernel_spmd as _run

    def flat(a):
        return _np.ascontiguousarray(_np.asarray(a))

    g = inputs
    W = {
        "ids": flat(_np.asarray(g["x"]).reshape(NT, P).T),
        "tok_W": flat(_np.asarray(g["L0_tok_W"]).T),
        "const": constants(),
    }
    for n in (0, 1):
        W[f"L{n}_Wqk"] = flat(_np.concatenate([_np.asarray(g[f"L{n}_attn_Wq"]).T, _np.asarray(g[f"L{n}_attn_Wk"]).T], axis=1))
        W[f"L{n}_Wv"] = flat(_np.asarray(g[f"L{n}_attn_Wv"]).T)
        W[f"L{n}_Wo"] = flat(_np.asarray(g[f"L{n}_attn_Wo"]).T)
    W["L2_Wqk"] = flat(_np.asarray(g["L1_ffn_W_qkv"])[:, :QK])
    W["L2_Wv"] = flat(_np.asarray(g["L1_ffn_W_qkv"])[:, QK:])
    W["L2_Wo"] = flat(g["L1_ffn_W_proj"])
    W["L2_bias"] = flat(g["L1_ffn_b_proj"])
    W["g_info"] = flat(g["L1_ffn_g_info"])
    for key, name in (("up", "L0_ffn_{}_up"), ("dn", "L0_ffn_{}_down")):
        for w in "AB":
            a = _np.asarray(g[name.format(w)])
            W[f"{key}_{w}"] = flat(a.transpose(2, 0, 1).reshape(a.shape[2], -1))
        W[f"{key}_W"] = flat(_np.asarray(g[name.format("W")]).T)
        W[f"{key}_bias"] = flat(g[name.format("bias")])
        W[f"{key}_scale"] = flat(g[name.format("scale")])
    nc = _bacc.Bacc("TRN2", target_bir_lowering=False, num_devices=1)
    T = {n: nc.dram_tensor(n, shape, dt, kind="ExternalInput").ap() for n, (shape, dt) in INPUTS.items()}
    out = nc.dram_tensor("out", (BATCH, SEQ, D), F32, kind="ExternalOutput").ap()
    tower(nc, T, out)
    r = _run(nc, [W], core_ids=[0])
    return r.results[0]["out"]
```
